# Optimizing a Trainium2 kernel written in Bass

```python
import numpy as np
import jax
import jax.numpy as jnp

def _softmax(x, axis=-1):
    return jax.nn.softmax(x, axis=axis)

def _gelu(x):
    return jax.nn.gelu(x, approximate=True)

def _silu(x):
    return jax.nn.silu(x)

def _sigmoid(x):
    return jax.nn.sigmoid(x)

def _layernorm(x, axis=-1, eps=1e-05):
    m = jnp.mean(x, axis=axis, keepdims=True)
    v = jnp.var(x, axis=axis, keepdims=True)
    return (x - m) / jnp.sqrt(v + eps)

def _scatter_add(tgt, idx, src, axis=0):
    return tgt.at[idx].add(src)

def _segment_sum(src, seg, n):
    return jax.ops.segment_sum(src, seg, n)
kernel_name = 'mk_macaron_d1_jaxref_r8_3406a5'

def setup_inputs(seed: int=0):
    np.random.seed(seed)
    _w = jnp.asarray

    def _L0_attn_setup():
        import jax, jax.numpy as jnp
        import numpy as np
        H = 16
        D = 64
        BQ = 64
        BKV = 64

        def _flash_tiled(q, k, v, scale):
            B, nh, S, d = q.shape
            nq, nkv = (S // BQ, S // BKV)
            qb = q.reshape(B, nh, nq, BQ, d)
            kb = k.reshape(B, nh, nkv, BKV, d).transpose(2, 0, 1, 3, 4)
            vb = v.reshape(B, nh, nkv, BKV, d).transpose(2, 0, 1, 3, 4)
            o0 = jnp.zeros((B, nh, nq, BQ, d), q.dtype)
            m0 = jnp.full((B, nh, nq, BQ), -jnp.inf, q.dtype)
            l0 = jnp.zeros((B, nh, nq, BQ), q.dtype)

            def step(carry, kv):
                o, m, l = carry
                kj, vj = kv
                s = jnp.einsum('bhnqd,bhkd->bhnqk', qb, kj) * scale
                m_new = jnp.maximum(m, s.max(axis=-1))
                p = jnp.exp(s - m_new[..., None])
                alpha = jnp.exp(m - m_new)
                l_new = alpha * l + p.sum(axis=-1)
                o_new = (alpha[..., None] * o + jnp.einsum('bhnqk,bhkd->bhnqd', p, vj)) / l_new[..., None]
                return ((o_new, m_new, l_new), None)
            (o, _, _), _ = jax.lax.scan(step, (o0, m0, l0), (kb, vb))
            return o.reshape(B, nh, S, d)
        key = jax.random.key(seed)
        ks = jax.random.split(key, 5)
        B, S, dim = (2, 256, 128)
        x = jax.random.normal(ks[0], (B, S, dim), dtype=jnp.float32)
        Wq = jax.random.normal(ks[1], (dim, H * D), dtype=jnp.float32) * 0.02
        Wk = jax.random.normal(ks[2], (dim, H * D), dtype=jnp.float32) * 0.02
        Wv = jax.random.normal(ks[3], (dim, H * D), dtype=jnp.float32) * 0.02
        Wo = jax.random.normal(ks[4], (H * D, dim), dtype=jnp.float32) * 0.02
        return {'x': x, 'Wq': Wq, 'Wk': Wk, 'Wv': Wv, 'Wo': Wo}
    _L0_attn_in = _L0_attn_setup()

    def _L0_ffn_setup():
        import jax, jax.numpy as jnp
        import numpy as np
        D = 128
        F = 128
        E = 8
        K = 2
        B, T = (2, 256)

        def _moe_forward(x, router_w, w1, w2, shared_gate_up, shared_down, shared_gate_w):
            b, t, d = x.shape
            xf = x.reshape(-1, d)
            n = xf.shape[0]
            logits = xf @ router_w
            probs = jax.nn.softmax(logits, axis=-1)
            topw, topi = jax.lax.top_k(probs, K)
            combine = jnp.zeros((n, E), dtype=probs.dtype).at[jnp.arange(n)[:, None], topi].add(topw)
            h = jax.nn.silu(jnp.einsum('nd,edf->nef', xf, w1))
            ye = jnp.einsum('nef,efd->ned', h, w2)
            routed = jnp.einsum('ne,ned->nd', combine, ye)
            gu = xf @ shared_gate_up
            gate, up = (gu[:, :F], gu[:, F:])
            shared = jax.nn.silu(gate) * up @ shared_down
            shared = jax.nn.sigmoid(xf @ shared_gate_w) * shared
            return (routed + shared).reshape(b, t, d)
        key = jax.random.key(seed)
        ks = jax.random.split(key, 7)
        std = 0.02
        x = jax.random.normal(ks[0], (B, T, D), dtype=jnp.float32)
        router_w = jax.random.normal(ks[1], (D, E), dtype=jnp.float32) * std
        w1 = jax.random.normal(ks[2], (E, D, F), dtype=jnp.float32) * std
        w2 = jax.random.normal(ks[3], (E, F, D), dtype=jnp.float32) * std
        shared_gate_up = jax.random.normal(ks[4], (D, 2 * F), dtype=jnp.float32) * std
        shared_down = jax.random.normal(ks[5], (F, D), dtype=jnp.float32) * std
        shared_gate_w = jax.random.normal(ks[6], (D, 1), dtype=jnp.float32) * std
        return {'x': x, 'router_w': router_w, 'w1': w1, 'w2': w2, 'shared_gate_up': shared_gate_up, 'shared_down': shared_down, 'shared_gate_w': shared_gate_w}
    _L0_ffn_in = _L0_ffn_setup()
    _d = {'L0_attn_x': _L0_attn_in['x'], 'L0_attn_Wq': _L0_attn_in['Wq'], 'L0_attn_Wk': _L0_attn_in['Wk'], 'L0_attn_Wv': _L0_attn_in['Wv'], 'L0_attn_Wo': _L0_attn_in['Wo'], 'L0_ffn_router_w': _L0_ffn_in['router_w'], 'L0_ffn_w1': _L0_ffn_in['w1'], 'L0_ffn_w2': _L0_ffn_in['w2'], 'L0_ffn_shared_gate_up': _L0_ffn_in['shared_gate_up'], 'L0_ffn_shared_down': _L0_ffn_in['shared_down'], 'L0_ffn_shared_gate_w': _L0_ffn_in['shared_gate_w']}
    _x0 = _d['L0_attn_x']
    _d['L0_attn_x'] = jax.random.normal(jax.random.fold_in(jax.random.key(seed), 1), (4, 512, 128), dtype=_x0.dtype)
    del _x0
    return _d

def reference(L0_attn_x, L0_attn_Wq, L0_attn_Wk, L0_attn_Wv, L0_attn_Wo, L0_ffn_router_w, L0_ffn_w1, L0_ffn_w2, L0_ffn_shared_gate_up, L0_ffn_shared_down, L0_ffn_shared_gate_w):

    def _L0_attn_ref(x, Wq, Wk, Wv, Wo):
        import jax, jax.numpy as jnp
        import numpy as np
        H = 16
        D = 64
        BQ = 64
        BKV = 64

        def _flash_tiled(q, k, v, scale):
            B, nh, S, d = q.shape
            nq, nkv = (S // BQ, S // BKV)
            qb = q.reshape(B, nh, nq, BQ, d)
            kb = k.reshape(B, nh, nkv, BKV, d).transpose(2, 0, 1, 3, 4)
            vb = v.reshape(B, nh, nkv, BKV, d).transpose(2, 0, 1, 3, 4)
            o0 = jnp.zeros((B, nh, nq, BQ, d), q.dtype)
            m0 = jnp.full((B, nh, nq, BQ), -jnp.inf, q.dtype)
            l0 = jnp.zeros((B, nh, nq, BQ), q.dtype)

            def step(carry, kv):
                o, m, l = carry
                kj, vj = kv
                s = jnp.einsum('bhnqd,bhkd->bhnqk', qb, kj) * scale
                m_new = jnp.maximum(m, s.max(axis=-1))
                p = jnp.exp(s - m_new[..., None])
                alpha = jnp.exp(m - m_new)
                l_new = alpha * l + p.sum(axis=-1)
                o_new = (alpha[..., None] * o + jnp.einsum('bhnqk,bhkd->bhnqd', p, vj)) / l_new[..., None]
                return ((o_new, m_new, l_new), None)
            (o, _, _), _ = jax.lax.scan(step, (o0, m0, l0), (kb, vb))
            return o.reshape(B, nh, S, d)
        B, S, dim = x.shape
        scale = D ** (-0.5)
        q = (x @ Wq).reshape(B, S, H, D).transpose(0, 2, 1, 3)
        k = (x @ Wk).reshape(B, S, H, D).transpose(0, 2, 1, 3)
        v = (x @ Wv).reshape(B, S, H, D).transpose(0, 2, 1, 3)
        o = _flash_tiled(q, k, v, scale)
        out = o.transpose(0, 2, 1, 3).reshape(B, S, H * D)
        return out @ Wo

    def _L0_ffn_ref(x, router_w, w1, w2, shared_gate_up, shared_down, shared_gate_w):
        import jax, jax.numpy as jnp
        import numpy as np
        D = 128
        F = 128
        E = 8
        K = 2
        B, T = (2, 256)

        def _moe_forward(x, router_w, w1, w2, shared_gate_up, shared_down, shared_gate_w):
            b, t, d = x.shape
            xf = x.reshape(-1, d)
            n = xf.shape[0]
            logits = xf @ router_w
            probs = jax.nn.softmax(logits, axis=-1)
            topw, topi = jax.lax.top_k(probs, K)
            combine = jnp.zeros((n, E), dtype=probs.dtype).at[jnp.arange(n)[:, None], topi].add(topw)
            h = jax.nn.silu(jnp.einsum('nd,edf->nef', xf, w1))
            ye = jnp.einsum('nef,efd->ned', h, w2)
            routed = jnp.einsum('ne,ned->nd', combine, ye)
            gu = xf @ shared_gate_up
            gate, up = (gu[:, :F], gu[:, F:])
            shared = jax.nn.silu(gate) * up @ shared_down
            shared = jax.nn.sigmoid(xf @ shared_gate_w) * shared
            return (routed + shared).reshape(b, t, d)
        return _moe_forward(x, router_w, w1, w2, shared_gate_up, shared_down, shared_gate_w)
    x = L0_attn_x
    x = x + 0.5 * _L0_ffn_ref(_layernorm(x, axis=-1), L0_ffn_router_w, L0_ffn_w1, L0_ffn_w2, L0_ffn_shared_gate_up, L0_ffn_shared_down, L0_ffn_shared_gate_w)
    x = x + _L0_attn_ref(_layernorm(x, axis=-1), L0_attn_Wq, L0_attn_Wk, L0_attn_Wv, L0_attn_Wo)
    x = x + 0.5 * _L0_ffn_ref(_layernorm(x, axis=-1), L0_ffn_router_w, L0_ffn_w1, L0_ffn_w2, L0_ffn_shared_gate_up, L0_ffn_shared_down, L0_ffn_shared_gate_w)
    return x

_drawn_inputs = setup_inputs


def setup_inputs(seed=0):
    import zlib

    import numpy as np

    out = dict(_drawn_inputs(seed))
    spreads = {}
    factors = {'L0_attn_Wq': 8.0,
     'L0_attn_Wk': 8.0,
     'L0_attn_Wv': 8.0,
     'L0_attn_Wo': 8.0,
     'L0_ffn_router_w': 8.0,
     'L0_ffn_w1': 8.0,
     'L0_ffn_w2': 8.0,
     'L0_ffn_shared_gate_up': 8.0,
     'L0_ffn_shared_down': 8.0,
     'L0_ffn_shared_gate_w': 8.0}
    for name, (base, spread) in spreads.items():
        noise = np.random.default_rng([zlib.crc32(name.encode()), seed]).standard_normal(out[name].shape)
        drawn = base * np.exp(spread * noise) if base else spread * noise
        out[name] = jnp.asarray(drawn.astype(out[name].dtype))
    for name, factor in factors.items():
        out[name] = (out[name] * factor).astype(out[name].dtype)
    return out
```

```python
import concourse.bass as bass
from concourse import mybir
from contextlib import ExitStack


def macaron_kernel(nc, x_in, wq_in, wk_in, wv_in, wo_in, router_in, w1_in, w2_in, gate_up_in,
                   down_in, shared_gate_in, out):
    fp32 = mybir.dt.float32
    fp32r = mybir.dt.float32r
    int32 = mybir.dt.int32
    ALU = mybir.AluOpType
    ACT = mybir.ActivationFunctionType
    AX = mybir.AxisListType
    ds = bass.ds

    B, S, D = x_in.shape
    E, _, F = w1_in.shape
    HD = 64
    H = wq_in.shape[1] // HD
    BLK = 64
    P = 128
    QT = S // P
    NBLK = S // BLK
    PAIRS = H // 2
    UNITS = B * H
    NE = E + 1
    NH = NE + 1
    EPS = 1e-5
    RSQRT_SEED = float(0x5F3759DF)
    FAR = -3.0e38
    TINY = 2.0 ** -60
    CR = HD + 2 * NBLK

    ctx = ExitStack()
    with ctx:
        def sb(name, shape, dt=fp32):
            return ctx.enter_context(nc.sbuf_tensor(name, shape, dt))

        def sem(name):
            return ctx.enter_context(nc.semaphore(name))

        x = sb("x", [P, B * QT * D])
        xT_hi = sb("xT_hi", [D, B * S], fp32r)
        xT_lo = sb("xT_lo", [D, B * S], fp32r)
        w1_hi = sb("w1_hi", [D, NH * F], fp32r)
        w1_lo = sb("w1_lo", [D, NH * F], fp32r)
        w2 = sb("w2", [F, NE * D])
        router_hi = sb("router_hi", [D, P], fp32r)
        router_lo = sb("router_lo", [D, P], fp32r)
        wqkv = sb("wqkv", [D, 3, H * HD])
        wo = sb("wo", [2 * HD, PAIRS * D])
        oT = sb("oT", [2 * HD, B * PAIRS * S])
        w_raw = oT[:, 0:NH * F]
        router_raw = oT[:, 2048:2048 + P]
        sel_raw = oT[:, 4096:4096 + NE * P]
        block_raw = oT[HD:CR, 8192:8192 + S]
        oT_raw = oT[:, 10240:10240 + S]
        xs_hi = sb("xs_hi", [D, S], fp32r)
        xs_lo = sb("xs_lo", [D, S], fp32r)
        w_hi = sb("w_hi", [D, 3, P], fp32r)
        w_lo = sb("w_lo", [D, 3, P], fp32r)
        q_pair = sb("q_pair", [P, 2, S], fp32r)
        k_pair = sb("k_pair", [P, 2, S], fp32r)
        NU = 4
        q_hh = [sb(f"q_hh{n}", [2 * HD, S], fp32r) for n in range(NU)]
        k_hl = [sb(f"k_hl{n}", [2 * HD, S], fp32r) for n in range(NU)]
        q_lc = [sb(f"q_lc{n}", [CR, S], fp32r) for n in range(NU)]
        k_hb = [sb(f"k_hb{n}", [CR, S], fp32r) for n in range(NU)]
        v_st = [sb(f"v_st{n}", [P, QT, P]) for n in range(2)]
        e_sb = sb("e_sb", [P, 2, 2 * S])
        half = sb("half", [P, 2, 2 * NBLK, BLK // 2])
        pT = sb("pT", [P, QT, S])
        th = e_sb[:, 0, :].rearrange("p (n s) -> p n s", n=2)
        tmp = e_sb[:, 1, :].rearrange("p (n s) -> p n s", n=2)
        hc = pT
        xn = half[:, :, :, :].rearrange("p a b c -> p (a b c)")[:, 0:QT * D]
        ident = sb("ident", [P, P])
        sel = sb("sel", [P, NE * P], fp32r)
        combT = sb("combT", [P, 2 * S], fp32r)
        logitT = sb("logitT", [NE, S])
        stats = sb("stats", [P, QT, 6])
        rs = sb("rs", [P, 4, QT])
        rt = sb("rt", [P, 8, QT * 16])
        comb = sb("comb", [P, QT, 32])
        reset0 = sb("reset0", [P, QT * NBLK])
        reset1 = sb("reset1", [P, QT * NBLK])
        far0 = sb("far0", [P, QT * NBLK])
        bmax = sb("bmax", [P, QT * NBLK])
        bsum = sb("bsum", [P, QT * NBLK])
        nm = sb("nm", [P, 2, QT])
        st = sb("st", [P, 5, QT * NBLK])
        ctile = sb("ctile", [P, QT, CR])

        psA = ctx.enter_context(nc.psum_tensor("psA", [P, 4, S], fp32))
        psB = [ctx.enter_context(nc.psum_tensor(f"psB{n}", [P, S], fp32)) for n in range(2)]
        psY = ctx.enter_context(nc.psum_tensor("psY", [P, S], fp32))
        psM = ctx.enter_context(nc.psum_tensor("psM", [P, S], fp32))

        x_in_s = sem("x_in_s"); w_in_s = sem("w_in_s"); wa_in_s = sem("wa_in_s")
        r_zero_s = sem("r_zero_s"); r_in_s = sem("r_in_s")
        consts_s = sem("consts_s"); pool_step = sem("pool_step"); split_s = sem("split_s")
        dve_step = sem("dve_step")
        xn_s = sem("xn_s"); xT_ps = sem("xT_ps"); xT_hi_s = sem("xT_hi_s"); xT_lo_s = sem("xT_lo_s")
        logit_ps = sem("logit_ps"); logitT_s = sem("logitT_s"); lt_ps = sem("lt_ps")
        rexp_in = sem("rexp_in"); rexp_s = sem("rexp_s")
        comb_s = sem("comb_s"); combT_ps = sem("combT_ps"); combT_s = sem("combT_s")
        hid_ps = sem("hid_ps"); th_s = sem("th_s"); hid_used = sem("hid_used")
        cb_ps = sem("cb_ps"); hc_s = sem("hc_s"); y_ps = sem("y_ps"); x_s = sem("x_s")
        xs_s = sem("xs_s"); wp_s = sem("wp_s")
        q_ps = sem("q_ps"); q_hi_s = sem("q_hi_s"); q_lo_s = sem("q_lo_s")
        k_ps = sem("k_ps"); k_hi_s = sem("k_hi_s"); k_lo_s = sem("k_lo_s")
        v_ps = sem("v_ps"); v_s = sem("v_s"); qk_s = sem("qk_s")
        s_ps = sem("s_ps"); nm_s = sem("nm_s"); e_s = sem("e_s"); half_s = sem("half_s")
        bsum_s = sem("bsum_s"); ln_in = sem("ln_in"); ln_s = sem("ln_s")
        c_s = sem("c_s"); cT_ps = sem("cT_ps"); cT_s = sem("cT_s")
        sT_ps = sem("sT_ps"); pT_s = sem("pT_s"); pv_s = sem("pv_s"); o_ps = sem("o_ps")
        o_s = sem("o_s"); zT_ps = sem("zT_ps"); zT_s = sem("zT_s"); z_ps = sem("z_ps")
        z_s = sem("z_s"); out_s = sem("out_s")

        block = ctx.enter_context(nc.Block())

        QK_DMAS = 12
        FFN_LAG = 2

        def raw(ap):
            return ap.bitcast(fp32)

        def loop_units(eng, slot):
            slot(-1, -1, UNITS)
            with eng.Fori(0, UNITS // NU - 1) as i:
                for s in range(NU):
                    slot(i * NU + s, s, UNITS)
            for s in range(NU):
                slot(UNITS - NU + s, s, UNITS - NU + s)

        def pair_of(u, s):
            return (u - s % 2) // 2

        @block.sync
        def _(sp):
            xv = x[:, :].rearrange("p (t d) -> p t d", d=D)
            for b in range(B):
                sp.dma_start(xv[:, b * QT:(b + 1) * QT, :],
                             x_in[b].rearrange("(t p) d -> p t d", p=P)).then_inc(x_in_s, 16)
            sp.dma_start(wo[:, :].rearrange("r (h d) -> r h d", d=D),
                         wo_in.rearrange("(h r) d -> r h d", r=2 * HD)).then_inc(wa_in_s, 16)
            for n, w in enumerate((wq_in, wk_in, wv_in)):
                sp.dma_start(wqkv[:, n, :], w).then_inc(wa_in_s, 16)

            def copies(n, p):
                sp.wait_ge(q_hi_s, p + 1)
                for h in range(2):
                    for half_ in range(2):
                        sp.dma_start(raw(q_hh[n + h][half_ * HD:(half_ + 1) * HD, :]),
                                     raw(q_pair[h * HD:(h + 1) * HD, 0, :])).then_inc(qk_s, 16)
                sp.wait_ge(q_lo_s, p + 1)
                for h in range(2):
                    sp.dma_start(raw(q_lc[n + h][0:HD, :]), raw(q_pair[h * HD:(h + 1) * HD, 1, :]))\
                      .then_inc(qk_s, 16)
                sp.wait_ge(k_hi_s, p + 1)
                for h in range(2):
                    sp.dma_start(raw(k_hl[n + h][0:HD, :]), raw(k_pair[h * HD:(h + 1) * HD, 0, :]))\
                      .then_inc(qk_s, 16)
                    sp.dma_start(raw(k_hb[n + h][0:HD, :]), raw(k_pair[h * HD:(h + 1) * HD, 0, :]))\
                      .then_inc(qk_s, 16)
                sp.wait_ge(k_lo_s, p + 1)
                for h in range(2):
                    sp.dma_start(raw(k_hl[n + h][HD:2 * HD, :]), raw(k_pair[h * HD:(h + 1) * HD, 1, :]))\
                      .then_inc(qk_s, 16)

            def load_xs(b):
                sp.wait_ge(xT_hi_s, B + 1 + b)
                sp.wait_ge(xT_lo_s, B + 1 + b)
                sp.dma_start(raw(xs_hi[:, :]), raw(xT_hi[:, ds(b * S, S)])).then_inc(xs_s, 16)
                sp.dma_start(raw(xs_lo[:, :]), raw(xT_lo[:, ds(b * S, S)])).then_inc(xs_s, 16)

            def slot(u, s, last):
                if s == -1:
                    load_xs(0)
                    copies(0, 0)
                elif last != UNITS - 1 and s % 2 == 0 and last != UNITS - 2:
                    p = pair_of(u, s) + 1
                    if s == 2:
                        sp.wait_ge(v_ps, p)
                        load_xs((u + 2) // H)
                    copies(2 if s == 0 else 0, p)

            loop_units(sp, slot)
            for b in range(B):
                sp.wait_ge(x_s, 1 + B + b + 1)
                sp.dma_start(out[b].rearrange("(t p) d -> p t d", p=P),
                             xv[:, b * QT:(b + 1) * QT, :]).then_inc(out_s, 16)
            sp.wait_ge(out_s, 16 * B)

        @block.gpsimd
        def _(pool):
            for started in (hid_used, hc_s, x_s, y_ps, o_s, z_s):
                pool.sem_inc(started, 1)
            steps = [0]

            def step(ins):
                steps[0] += 1
                ins.then_inc(pool_step, 1)
                pool.wait_ge(pool_step, steps[0])

            for tile, value in ((ident[:, :], 0.0), (sel_raw, 0.0), (reset0[:, :], 1.0),
                                (reset1[:, :], 1.0), (far0[:, :], 0.0), (raw(combT[:, :]), 0.0),
                                (ctile[:, :, :], 0.0), (block_raw, 0.0)):
                step(pool.memset(tile, value))
            pool.memset(router_raw, 0.0).then_inc(r_zero_s, 1)
            pool.wait_ge(r_zero_s, 1)
            step(pool.affine_select(out=ident[:, :], in_=ident[:, :], compare_op=ALU.not_equal, fill=1.0,
                                    base=0, pattern=[[-1, P]], channel_multiplier=1))
            selv = sel_raw[0:2 * NE, :].rearrange("r (e f) -> r e f", f=P)
            for twin in range(2):
                step(pool.affine_select(out=selv, in_=selv, compare_op=ALU.not_equal, fill=1.0,
                                        base=twin * NE, pattern=[[1, NE], [0, P]],
                                        channel_multiplier=-1))
            blv = block_raw.rearrange("r (j k) -> r j k", k=BLK)
            for twin in range(2):
                step(pool.affine_select(out=blv, in_=blv, compare_op=ALU.not_equal, fill=1.0,
                                        base=twin * NBLK, pattern=[[1, NBLK], [0, BLK]],
                                        channel_multiplier=-1))
            for tile, at, value in ((reset0, 0, 0.0), (reset1, NBLK - 1, 0.0), (far0, 0, FAR)):
                tv = tile[:, :].rearrange("p (t j) -> p t j", j=NBLK)
                step(pool.memset(tv[:, :, at:at + 1], value))
            pool.tensor_copy(sel[:, :], sel_raw).then_inc(consts_s, 1)
            pool.wait_ge(consts_s, 1)
            for n in range(NU):
                pool.tensor_copy(k_hb[n][HD:CR, :], block_raw).then_inc(consts_s, 1)
                pool.wait_ge(consts_s, n + 2)

            def split_weights(p):
                pool.wait_ge(v_ps, p)
                src = wqkv[:, :, ds((p % PAIRS) * P, P)]
                pool.tensor_copy(w_hi[:, :, :], src).then_inc(wp_s, 1)
                return src

            def split_rest(p, src):
                pool.tensor_tensor(w_lo[:, :, :], src, w_hi[:, :, :].bitcast(fp32), ALU.subtract)\
                    .then_inc(wp_s, 1)

            def half_sums(u, n_first, split, p):
                for g in range(2):
                    if g == 1 and split is not None:
                        split_rest(p, split)
                    if g == 0 and split is not None:
                        pool.wait_ge(wp_s, 2 * p + 1)
                    pool.wait_ge(e_s, 2 * (u + 1) + g + 1)
                    if not n_first:
                        pool.wait_ge(bsum_s, 2 * u + g + 1)
                    ev = e_sb[:, g, :].rearrange("p (j k) -> p j k", k=BLK)
                    pool.tensor_tensor(half[:, g, :, :], ev[:, :, 0:BLK // 2], ev[:, :, BLK // 2:BLK],
                                       ALU.add).then_inc(half_s, 1)

            def slot(u, s, last):
                split, p = None, 0
                if s == -1:
                    pool.wait_ge(wa_in_s, 16 * 4)
                    src = split_weights(0)
                    pool.wait_ge(wp_s, 1)
                    split_rest(0, src)
                elif s % 2 == 0 and last != UNITS - 2:
                    p = pair_of(u, s) + 1
                    split = split_weights(p)
                if last != UNITS - 1:
                    half_sums(u, s == -1, split, p)

            loop_units(pool, slot)

        @block.scalar
        def _(act):
            act.wait_ge(r_zero_s, 1)
            act.dma_start(router_raw[:, 0:E], router_in).then_inc(r_in_s, 16)
            act.dma_start(router_raw[:, E:NE], shared_gate_in).then_inc(r_in_s, 16)
            act.dma_start(w_raw[:, 0:E * F].rearrange("d (e f) -> d e f", f=F),
                          w1_in.rearrange("e d f -> d e f")).then_inc(w_in_s, 16)
            act.dma_start(w_raw[:, E * F:NH * F], gate_up_in).then_inc(w_in_s, 16)
            act.dma_start(w2[:, 0:E * D].rearrange("f (e d) -> f e d", d=D),
                          w2_in.rearrange("e f d -> f e d")).then_inc(w_in_s, 16)
            act.dma_start(w2[:, E * D:NE * D], down_in).then_inc(w_in_s, 16)

            def turned(n, b):
                act.wait_ge(xT_ps, n + 1)
                nc.scalar.activation(xT_hi[:, ds(b * S, S)], psM[:, :], ACT.Copy).then_inc(xT_hi_s, 1)

            def logits(g):
                act.wait_ge(logit_ps, g + 1)
                nc.scalar.activation(logitT[:, :], psM[0:NE, :], ACT.Copy).then_inc(logitT_s, 1)

            def router_exp(g):
                act.wait_ge(rexp_in, g + 1)
                lv = rt[:, 1, :].rearrange("p (t e) -> p t e", e=16)
                nc.scalar.activation(lv[:, :, 0:E], lv[:, :, 0:E], ACT.Exp).then_inc(rexp_s, 1)
                nc.scalar.activation(lv[:, :, E:NE], lv[:, :, E:NE], ACT.Tanh, scale=0.5)\
                    .then_inc(rexp_s, 1)

            def weights_turned(g):
                act.wait_ge(combT_ps, g + 1)
                nc.scalar.activation(combT[0:2 * NE, ds((g % 2) * S, S)], psM[0:2 * NE, :], ACT.Copy)\
                    .then_inc(combT_s, 1)

            def ffn(phase):
                norm, g0 = (0, 0) if phase == 0 else (2 * B, B)

                def prep(n, g, b, part):
                    (lambda: turned(n, b), lambda: logits(g), lambda: router_exp(g),
                     lambda: weights_turned(g))[part]()

                def experts(b, last):
                    g = b + g0
                    for e in range(NE):
                        act.wait_ge(hid_ps, NH * g + e + 1)
                        act.wait_ge(hid_used, 1 + NH * g + (e - 1 if e >= 2 else 0))
                        nc.scalar.activation(th[:, e % 2, :], psA[:, e % 4, :], ACT.Tanh, scale=0.5)\
                            .then_inc(th_s, 1)
                        if not last and e in (1, 3, 7, 8):
                            prep(norm + b + 1, g + 1, b + 1, (1, 3, 7, 8).index(e))

                for part in range(4):
                    prep(norm, g0, 0, part)
                with act.Fori(0, B - 1) as b:
                    experts(b, False)
                experts(B - 1, True)

            act.wait_ge(w_in_s, 16 * 4)
            act.wait_ge(r_in_s, 32)
            nc.scalar.activation(router_hi[:, :], router_raw, ACT.Copy).then_inc(split_s, 1)
            nc.scalar.activation(w1_hi[:, :], w_raw, ACT.Copy).then_inc(split_s, 1)
            ffn(0)

            with act.Fori(0, B) as b:
                turned(B + b, b)

            act.preload_act_table_set("natural_log_exp_and_others")

            def slot(u, s, last):
                n = u + 1
                project = (s % 2 == 0 and last != UNITS - 2) or s == -1
                p = 0 if s == -1 else pair_of(u, s) + 1
                stage1 = last != UNITS - 1
                stage2 = s != -1

                def exps(g):
                    act.wait_ge(nm_s, 2 * n + g + 1)
                    if s != -1:
                        act.wait_ge(half_s, 2 * u + g + 1)
                    for q in range(2):
                        ins = nc.scalar.activation(e_sb[:, g, q * S:(q + 1) * S], psA[:, 2 * g + q, :],
                                                   ACT.Exp, bias=nm[:, 0, 2 * g + q:2 * g + q + 1])
                    ins.then_inc(e_s, 1)

                def weighted(k):
                    act.wait_ge(sT_ps, QT * u + k + 1)
                    nc.scalar.activation(pT[:, k, :], psB[k % 2][:, :], ACT.Exp).then_inc(pT_s, 1)

                def q_hi():
                    act.wait_ge(q_ps, p + 1)
                    if s != -1:
                        act.wait_ge(qk_s, 16 * QK_DMAS * p)
                    nc.scalar.activation(q_pair[:, 0, :], psM[:, :], ACT.Copy, scale=HD ** -0.5)\
                        .then_inc(q_hi_s, 1)

                def k_hi():
                    act.wait_ge(k_ps, p + 1)
                    nc.scalar.activation(k_pair[:, 0, :], psM[:, :], ACT.Copy).then_inc(k_hi_s, 1)

                def v_out():
                    act.wait_ge(v_ps, p + 1)
                    nc.scalar.activation(v_st[(s // 2 + 1) % 2 if s != -1 else 0][:, :, :]
                                         .rearrange("p t d -> p (t d)"),
                                         psM[:, :], ACT.Copy).then_inc(v_s, 1)

                if s == -1:
                    q_hi(); k_hi(); v_out()
                if stage1:
                    exps(0)
                if stage2:
                    weighted(0); weighted(1)
                if stage1:
                    exps(1)
                if project and s != -1:
                    q_hi()
                if stage2:
                    weighted(2)
                if project and s != -1:
                    k_hi()
                if stage2:
                    weighted(3)
                if project and s != -1:
                    v_out()
                if stage1:
                    act.wait_ge(ln_in, n + 1)
                    nc.scalar.activation(st[:, 2, :], st[:, 2, :], ACT.Ln).then_inc(ln_s, 1)
                if stage2:
                    rows = slice((s % 2) * HD, (s % 2 + 1) * HD)
                    act.wait_ge(o_ps, u + 1)
                    nc.scalar.activation(oT[rows, ds(pair_of(u, s) * S, S)], psY[rows, :], ACT.Copy)\
                        .then_inc(o_s, 1)
                if stage1:
                    act.wait_ge(cT_ps, n + 1)
                    nc.scalar.activation(q_lc[(s + 1) % NU][HD:CR, :], psM[HD:CR, :], ACT.Copy)\
                        .then_inc(cT_s, 1)

            loop_units(act, slot)

            def zT(b, n):
                act.wait_ge(zT_ps, b + 1)
                nc.scalar.activation(pT[:, n, :], psA[:, n, :], ACT.Copy).then_inc(zT_s, 1)
            with act.Fori(0, B - 1, 2) as b:
                for n in range(2):
                    zT(b + n, n)
            ffn(1)

        @block.vector
        def _(dve):
            base, at, turn = [0], [0], [None, 0]

            def step(ins):
                at[0] += 1
                ins.then_inc(dve_step, 1)
                if turn[0] is None:
                    dve.wait_ge(dve_step, base[0] + at[0])
                else:
                    dve.wait_ge(dve_step, turn[0] * turn[1] + (base[0] + at[0]))

            def loop(first, count, stride, steps, body):
                base[0] += at[0]
                at[0] = 0
                with dve.Fori(first, first + count * stride, stride) as i:
                    turn[:] = [i if stride == 1 else i // stride, steps]
                    body(i)
                assert at[0] == steps, (at[0], steps)
                turn[0] = None
                base[0] += steps * count
                at[0] = 0

            V = nc.vector

            def norm(b):
                xb = [x[:, ds(b * (QT * D) + t * D, D)] for t in range(QT)]
                for t in range(QT):
                    ins = V.bn_stats(stats[:, t, :], xb[t])
                step(ins)
                me, qe, mo, qo = (stats[:, :, k] for k in (1, 2, 4, 5))
                mean, var, y, a = (rs[:, k, :] for k in range(4))
                V.tensor_tensor(a, me, mo, ALU.subtract)
                V.tensor_tensor(mean, me, mo, ALU.add)
                step(V.tensor_tensor(var, qe, qo, ALU.add))
                V.scalar_tensor_tensor(a, a, 0.25, a, ALU.mult, ALU.mult)
                V.tensor_scalar(mean, mean, 0.5, None, ALU.mult)
                step(V.tensor_scalar(var, var, 1.0 / D, EPS, ALU.mult, ALU.add))
                step(V.tensor_tensor(var, var, a, ALU.add))
                step(V.tensor_scalar(y.bitcast(int32), var.bitcast(int32), -0.5, RSQRT_SEED,
                                     ALU.mult, ALU.add))
                for _ in range(3):
                    step(V.scalar_tensor_tensor(a, y, -0.5, var, ALU.mult, ALU.mult))
                    step(V.tensor_tensor(a, a, y, ALU.mult))
                    step(V.scalar_tensor_tensor(y, a, 1.5, y, ALU.add, ALU.mult))
                for t in range(QT):
                    ins = V.tensor_scalar(xn[:, t * D:(t + 1) * D], xb[t], mean[:, t:t + 1],
                                          y[:, t:t + 1], ALU.subtract, ALU.mult)
                ins.then_inc(xn_s, 1)
            NORM_STEPS = 5 + 9

            def turned_lo(n, b):
                dve.wait_ge(xT_hi_s, n + 1)
                V.tensor_tensor(xT_lo[:, ds(b * S, S)], psM[:, :],
                                xT_hi[:, ds(b * S, S)].bitcast(fp32), ALU.subtract).then_inc(xT_lo_s, 1)

            def small(n):
                return rt[:, n, :].rearrange("p (t e) -> p t e", e=16)

            def router(g):
                logit, ls, m, pc, sel1, sel2, w = (small(n) for n in range(7))
                r8 = reset0[:, :].rearrange("p (t j) -> p t j", j=NBLK)
                dve.wait_ge(lt_ps, g + 1)
                step(V.tensor_copy(logit[:, :, 0:NE],
                                   psM[:, 0:QT * 16].rearrange("p (t e) -> p t e", e=16)[:, :, 0:NE]))
                step(V.tensor_reduce(m[:, :, 8:9], logit[:, :, 0:E], AX.X, ALU.max))
                V.tensor_copy(ls[:, :, E:NE], logit[:, :, E:NE])
                V.tensor_tensor(w[:, :, 0:E], logit[:, :, 0:E],
                                m[:, :, 8:9].broadcast_to([P, QT, E]), ALU.subtract)
                V.tensor_tensor(ls[:, :, 0:E], logit[:, :, 0:E],
                                m[:, :, 8:9].broadcast_to([P, QT, E]), ALU.subtract).then_inc(rexp_in, 1)
                dve.wait_ge(rexp_in, g + 1)

                def first_of(dst, mask):
                    for t in range(QT):
                        ins = V.tensor_tensor_scan(pc[:, t, 0:E], reset_one[:, 0:E], mask[:, t, 0:E],
                                                   0.0, ALU.mult, ALU.add)
                    step(ins)
                    step(V.scalar_tensor_tensor(dst[:, :, 0:E], pc[:, :, 0:E], 1.0, mask[:, :, 0:E],
                                                ALU.is_equal, ALU.mult))

                step(V.tensor_scalar(m[:, :, 0:E], w[:, :, 0:E], 0.0, None, ALU.is_equal))
                first_of(sel1, m)
                step(V.scalar_tensor_tensor(w[:, :, 0:E], sel1[:, :, 0:E], FAR, w[:, :, 0:E],
                                            ALU.mult, ALU.add))
                step(V.tensor_reduce(m[:, :, 8:9], w[:, :, 0:E], AX.X, ALU.max))
                step(V.tensor_tensor(m[:, :, 0:E], w[:, :, 0:E],
                                     m[:, :, 8:9].broadcast_to([P, QT, E]), ALU.is_equal))
                first_of(sel2, m)
                step(V.tensor_tensor(sel1[:, :, 0:E], sel1[:, :, 0:E], sel2[:, :, 0:E], ALU.add))
                dve.wait_ge(rexp_s, 2 * g + 2)
                step(V.tensor_reduce(m[:, :, 8:9], ls[:, :, 0:E], AX.X, ALU.add))
                step(V.reciprocal(m[:, :, 9:10], m[:, :, 8:9]))
                step(V.scalar_tensor_tensor(w[:, :, 0:E], ls[:, :, 0:E], 0.25, sel1[:, :, 0:E],
                                            ALU.mult, ALU.mult))
                V.tensor_tensor(w[:, :, 0:E], w[:, :, 0:E],
                                m[:, :, 9:10].broadcast_to([P, QT, E]), ALU.mult)
                step(V.tensor_scalar(w[:, :, E:NE], ls[:, :, E:NE], 0.125, 0.125, ALU.mult, ALU.add))
                step(V.tensor_copy(comb[:, :, 0:NE].bitcast(fp32r), w[:, :, 0:NE]))
                V.tensor_tensor(comb[:, :, NE:2 * NE], w[:, :, 0:NE], comb[:, :, 0:NE],
                                ALU.subtract).then_inc(comb_s, 1)
            ROUTER_STEPS = 2 + 1 + 2 + 3 + 2 + 1 + 5

            reset_one = rt[:, 7, :]

            def ffn(phase):
                norm0, g0 = (0, 0) if phase == 0 else (2 * B, B)

                def experts(b, last):
                    g = b + g0
                    for e in range(NE + 1):
                        if e < NE:
                            dve.wait_ge(th_s, NE * g + e + 1)
                            dve.wait_ge(hc_s, 1 + NE * g + (e - 1 if e >= 2 else 0))
                            V.scalar_tensor_tensor(tmp[:, e % 2, :], th[:, e % 2, :], 1.0,
                                                   psA[:, e % 4, :], ALU.add, ALU.mult)\
                             .then_inc(hid_used, 1)
                        if e == NE - 1:
                            dve.wait_ge(hid_ps, NH * g + NH)
                            dve.wait_ge(hid_used, 1 + NH * g + NE)
                            V.tensor_tensor(tmp[:, e % 2, :], tmp[:, e % 2, :],
                                            psA[:, (e + 1) % 4, :], ALU.mult).then_inc(hid_used, 1)
                        if e >= 1:
                            k = e - 1
                            dve.wait_ge(cb_ps, NE * g + k + 1)
                            dve.wait_ge(hid_used, 1 + NH * g + (k + 1 if k < NE - 1 else NH))
                            dve.wait_ge(y_ps, 1 + NE * g + (k - 2 if k >= 3 else 0))
                            V.tensor_tensor(hc[:, k % 3, :], tmp[:, k % 2, :], psB[k % 2][:, :],
                                            ALU.mult).then_inc(hc_s, 1)
                        if not last and e == 1:
                            norm(b + 1)
                        if not last and e == 3:
                            turned_lo(norm0 + b + 1, b + 1)
                        if not last and e == 7:
                            router(g + 1)
                    dve.wait_ge(y_ps, 1 + NE * (g + 1))
                    xb = x[:, ds(b * (QT * D), QT * D)]
                    V.tensor_tensor(xb, xb, psY[:, :], ALU.add).then_inc(x_s, 1)

                if phase == 0:
                    dve.wait_ge(x_in_s, 16 * B)
                norm(0)
                turned_lo(norm0, 0)
                router(g0)
                loop(0, B - 1, 1, NORM_STEPS + ROUTER_STEPS, lambda b: experts(b, False))
                experts(B - 1, True)

            V.memset(rt[:, :, :], 0.0).then_inc(dve_step, 1)
            dve.wait_ge(dve_step, 1)
            base[0] = 1
            V.memset(comb[:, :, :], 0.0)
            step(V.memset(reset_one, 1.0))
            dve.wait_ge(split_s, 2)
            V.tensor_tensor(router_lo[:, :], router_raw, router_hi[:, :].bitcast(fp32), ALU.subtract)
            V.tensor_tensor(w1_lo[:, :], w_raw, w1_hi[:, :].bitcast(fp32), ALU.subtract)\
             .then_inc(split_s, 1)
            ffn(0)

            def ln2(b):
                dve.wait_ge(x_s, 1 + b + 1)
                norm(b)
                turned_lo(B + b, b)
            loop(0, B, 1, NORM_STEPS, ln2)

            tiles = lambda ap: ap.rearrange("p (t j) -> p t j", j=NBLK)

            def slot(u, s, last):
                n = u + 1
                project = (s % 2 == 0 and last != UNITS - 2) or s == -1
                p = 0 if s == -1 else pair_of(u, s) + 1

                def lows():
                    dve.wait_ge(q_hi_s, p + 1)
                    V.scalar_tensor_tensor(q_pair[:, 1, :], psM[:, :], HD ** -0.5,
                                           q_pair[:, 0, :].bitcast(fp32), ALU.mult, ALU.subtract)\
                     .then_inc(q_lo_s, 1)
                    dve.wait_ge(k_hi_s, p + 1)
                    V.tensor_tensor(k_pair[:, 1, :], psM[:, :], k_pair[:, 0, :].bitcast(fp32),
                                    ALU.subtract).then_inc(k_lo_s, 1)

                if s == -1:
                    lows()
                if last == UNITS - 1:
                    return
                neg = nm[:, 0, :]
                for g in range(2):
                    dve.wait_ge(s_ps, 2 * n + g + 1)
                    bm = tiles(bmax[:, :])[:, 2 * g:2 * g + 2, :]
                    step(V.tensor_reduce(bmax[:, g * 2 * NBLK:(g + 1) * 2 * NBLK],
                                         psA[:, 2 * g:2 * g + 2, :].rearrange("p t (j k) -> p (t j) k", k=BLK),
                                         AX.X, ALU.max))
                    V.tensor_reduce(nm[:, 0, 2 * g:2 * g + 2], bm, AX.X, ALU.max, negate=True)\
                     .then_inc(nm_s, 1)
                if project and s != -1:
                    lows()
                pm, dd, lsum, back, c = (st[:, k, :] for k in range(5))
                dve.wait_ge(nm_s, 2 * n + 2)
                step(V.tensor_tensor_scan(pm, far0[:, :], bmax[:, :], FAR, ALU.add, ALU.max))
                V.tensor_tensor(tiles(dd), tiles(pm),
                                neg.rearrange("p (t o) -> p t o", o=1).broadcast_to([P, QT, NBLK]),
                                ALU.add).then_inc(dve_step, 1)
                at[0] += 1
                for g in range(2):
                    dve.wait_ge(half_s, 2 * n + g + 1)
                    V.tensor_reduce(bsum[:, g * 2 * NBLK:(g + 1) * 2 * NBLK], half[:, g, :, :],
                                    AX.X, ALU.add).then_inc(bsum_s, 1)
                dve.wait_ge(bsum_s, 2 * n + 2)
                step(V.tensor_tensor_scan(lsum, reset0[:, :], bsum[:, :], 0.0, ALU.mult, ALU.add))
                V.tensor_scalar(lsum, lsum, TINY, None, ALU.max).then_inc(ln_in, 1)
                dve.wait_ge(ln_s, n + 1)
                step(V.tensor_tensor(lsum, lsum, dd, ALU.subtract))
                step(V.tensor_tensor_scan(back[:, ::-1], reset1[:, ::-1], lsum[:, ::-1], 0.0,
                                          ALU.mult, ALU.add))
                step(V.tensor_tensor(tiles(c), neg.rearrange("p (t o) -> p t o", o=1)
                                     .broadcast_to([P, QT, NBLK]), tiles(back), ALU.subtract))
                step(V.tensor_copy(ctile[:, :, HD:HD + NBLK].bitcast(fp32r), tiles(c)))
                V.tensor_tensor(ctile[:, :, HD + NBLK:CR], tiles(c), ctile[:, :, HD:HD + NBLK],
                                ALU.subtract).then_inc(c_s, 1)

            SLOT_STEPS = 2 + 2 + 1 + 4
            slot(-1, -1, UNITS)

            def turn4(i):
                for s in range(NU):
                    slot(i * NU + s, s, UNITS)
            loop(0, UNITS // NU - 1, 1, NU * SLOT_STEPS, turn4)
            for s in range(NU):
                slot(UNITS - NU + s, s, UNITS - NU + s)

            def add(b):
                for n in range(2):
                    dve.wait_ge(z_ps, b + n + 1)
                    xb = x[:, ds((b + n) * (QT * D), QT * D)]
                    V.tensor_tensor(xb, xb, psB[n][:, :], ALU.add).then_inc(z_s, 1)
            with dve.Fori(0, B - 1, 2) as b:
                add(b)
            dve.wait_ge(z_s, 1 + B)
            ffn(1)

        @block.tensor
        def _(pe):
            T = nc.tensor

            def three(o, w_hi_, w_lo_, r_hi, r_lo):
                T.matmul(o, w_hi_, r_hi, start=True, stop=False)
                T.matmul(o, w_hi_, r_lo, start=False, stop=False)
                return T.matmul(o, w_lo_, r_hi, start=False, stop=True)

            def turn_x(n, misc_free):
                pe.wait_ge(xn_s, n + 1)
                misc_free()
                for t in range(QT):
                    ins = T.transpose(psM[:, t * P:(t + 1) * P], xn[:, t * D:(t + 1) * D], ident[:, :])
                ins.then_inc(xT_ps, 1)

            def ffn(phase):
                norm0, g0 = (0, 0) if phase == 0 else (2 * B, B)

                def prep(n, g, b, part):
                    if part == 0:
                        turn_x(n, lambda: None if isinstance(g, int) and g == 0 else pe.wait_ge(combT_s, g))
                    if part == 1:
                        pe.wait_ge(xT_hi_s, n + 1)
                        pe.wait_ge(xT_lo_s, n + 1)
                        three(psM[:, :], router_hi[:, :], router_lo[:, :], xT_hi[:, ds(b * S, S)],
                              xT_lo[:, ds(b * S, S)]).then_inc(logit_ps, 1)
                    if part == 2:
                        for t in range(QT):
                            ins = T.transpose(psM[:, t * 16:t * 16 + NE],
                                              logitT[:, t * P:(t + 1) * P], ident[0:NE, 0:NE])
                        ins.then_inc(lt_ps, 1)
                    if part == 3:
                        pe.wait_ge(comb_s, g + 1)
                        for t in range(QT):
                            ins = T.transpose(psM[0:2 * NE, t * P:(t + 1) * P],
                                              comb[:, t, 0:2 * NE], ident[:, :])
                        ins.then_inc(combT_ps, 1)

                def hidden(b, j):
                    g = b + g0
                    pe.wait_ge(hid_used, 1 + NH * g + (j - 3 if j >= 4 else 0))
                    three(psA[:, j % 4, :], w1_hi[:, j * F:(j + 1) * F], w1_lo[:, j * F:(j + 1) * F],
                          xT_hi[:, ds(b * S, S)], xT_lo[:, ds(b * S, S)]).then_inc(hid_ps, 1)

                def combine(b, e):
                    g = b + g0
                    pe.wait_ge(hc_s, 1 + NE * g + (e - 1 if e >= 2 else 0))
                    pe.wait_ge(combT_s, g + 1)
                    T.matmul(psB[e % 2][:, :], sel[:, e * P:(e + 1) * P],
                             combT[:, ds((g % 2) * S, S)], start=True, stop=True).then_inc(cb_ps, 1)

                def second(b, e):
                    g = b + g0
                    pe.wait_ge(hc_s, 1 + NE * g + e + 1)
                    if e == 0:
                        pe.wait_ge(x_s, 1 + g)
                    for t in range(QT):
                        ins = T.matmul(psY[:, t * D:(t + 1) * D], hc[:, e % 3, t * P:(t + 1) * P],
                                       w2[:, e * D:(e + 1) * D], start=(e == 0 and t == 0),
                                       stop=(e == NE - 1 and t == QT - 1), skip_group_check=True)
                    ins.then_inc(y_ps, 1)

                def experts(b, last):
                    g = b + g0
                    for e in range(NE + FFN_LAG):
                        if e < NE:
                            hidden(b, e)
                            if e == NE - 1:
                                hidden(b, NE)
                            combine(b, e)
                        if not last and e == 6:
                            pe.wait_ge(logitT_s, g + 2)
                        if e >= FFN_LAG:
                            second(b, e - FFN_LAG)
                        if not last and e in (2, 4, 6, 10):
                            prep(norm0 + b + 1, g + 1, b + 1, (2, 4, 6, 10).index(e))

                for part in range(4):
                    if part == 2:
                        pe.wait_ge(logitT_s, g0 + 1)
                    prep(norm0, g0, 0, part)
                with pe.Fori(0, B - 1) as b:
                    experts(b, False)
                experts(B - 1, True)

            pe.wait_ge(consts_s, 1 + NU)
            pe.wait_ge(split_s, 3)
            pe.wait_ge(w_in_s, 16 * 4)
            ffn(0)

            def misc_free(b):
                pe.wait_ge(xT_lo_s, B + b)
                pe.wait_ge(xT_hi_s, B + b)
            with pe.Fori(0, B) as b:
                turn_x(B + b, lambda: misc_free(b))

            def slot(u, s, last):
                n = u + 1
                nb = (s + 1) % NU
                ub = s % NU
                project = (s % 2 == 0 and last != UNITS - 2) or s == -1
                p = 0 if s == -1 else pair_of(u, s) + 1
                stage1 = last != UNITS - 1
                stage2 = s != -1

                def scores(g):
                    if g == 0:
                        pe.wait_ge(qk_s, 16 * QK_DMAS * (p + 1 if project and s == -1 else
                                                         pair_of(u + 1, s + 1) + 1))
                    if s != -1:
                        pe.wait_ge(e_s, 2 * u + g + 1)
                    for q in (2 * g, 2 * g + 1):
                        T.matmul(psA[:, q, :], q_hh[nb][:, q * P:(q + 1) * P], k_hl[nb][:, :],
                                 start=True, stop=False)
                    for q in (2 * g, 2 * g + 1):
                        ins = T.matmul(psA[:, q, :], q_lc[nb][0:HD, q * P:(q + 1) * P],
                                       k_hl[nb][0:HD, :], start=False, stop=True)
                    ins.then_inc(s_ps, 1)

                def scoresT(ks):
                    for k in ks:
                        T.matmul(psB[k % 2][:, :], k_hl[ub][:, k * P:(k + 1) * P], q_hh[ub][:, :],
                                 start=True, stop=False)
                    if ks[0] == 0:
                        pe.wait_ge(cT_s, u + 1)
                    for k in ks:
                        T.matmul(psB[k % 2][:, :], k_hb[ub][:, k * P:(k + 1) * P], q_lc[ub][:, :],
                                 start=False, stop=True).then_inc(sT_ps, 1)

                def pv(k):
                    rows = slice((s % 2) * HD, (s % 2 + 1) * HD)
                    if k == 0:
                        pe.wait_ge(o_s, 1 + u)
                        pe.wait_ge(v_s, pair_of(u, s) + 1)
                    pe.wait_ge(pT_s, QT * u + k + 1)
                    ins = T.matmul(psY[rows, :], v_st[s // 2][:, k, rows], pT[:, k, :],
                                   start=(k == 0), stop=(k == QT - 1))
                    if k == QT - 1:
                        ins.then_inc(o_ps, 1)

                def project_qk(which, done):
                    if which == 0:
                        pe.wait_ge(wp_s, 2 * (p + 1))
                        if s == -1:
                            pe.wait_ge(xs_s, 32)
                            pe.wait_ge(xT_lo_s, 2 * B)
                        else:
                            pe.wait_ge(xs_s, 32 * ((p + 2) // 2))
                            pe.wait_ge(cT_s, u + 1)
                    else:
                        pe.wait_ge(q_hi_s, p + 1)
                        pe.wait_ge(q_lo_s, p + 1)
                    three(psM[:, :], w_hi[:, which, :], w_lo[:, which, :], xs_hi[:, :],
                          xs_lo[:, :]).then_inc(done, 1)

                def project_v():
                    pe.wait_ge(k_hi_s, p + 1)
                    pe.wait_ge(k_lo_s, p + 1)
                    for t in range(QT):
                        tt = slice(t * P, (t + 1) * P)
                        ins = three(psM[:, tt], xs_hi[:, tt], xs_lo[:, tt], w_hi[:, 2, :], w_lo[:, 2, :])
                    ins.then_inc(v_ps, 1)

                if s == -1:
                    project_qk(0, q_ps); project_qk(1, k_ps); project_v()
                if stage1:
                    scores(0)
                if stage2:
                    scoresT([0, 1])
                if project and s != -1:
                    project_qk(0, q_ps)
                if stage1:
                    scores(1)
                if stage2:
                    pv(0); scoresT([2])
                if project and s != -1:
                    project_qk(1, k_ps)
                if stage2:
                    pv(1); scoresT([3]); pv(2)
                if project and s != -1:
                    project_v()
                if stage2:
                    pv(3)
                if stage1:
                    pe.wait_ge(c_s, n + 1)
                    if project:
                        pe.wait_ge(v_s, p + 1)
                    for q in range(QT):
                        ins = T.transpose(psM[0:CR, q * P:(q + 1) * P], ctile[:, q, :], ident[:, :])
                    ins.then_inc(cT_ps, 1)

            loop_units(pe, slot)

            def output(b, n):
                pe.wait_ge(z_s, 1 + b)
                for h in range(PAIRS):
                    ins = T.matmul(psA[:, n, :], wo[:, h * D:(h + 1) * D],
                                   oT[:, ds(((b + n) * PAIRS + h) * S, S)],
                                   start=(h == 0), stop=(h == PAIRS - 1))
                ins.then_inc(zT_ps, 1)

            def back(b, n):
                pe.wait_ge(zT_s, b + n + 1)
                for t in range(QT):
                    ins = T.transpose(psB[n][:, t * P:(t + 1) * P], pT[:, n, t * P:(t + 1) * P],
                                      ident[:, :])
                ins.then_inc(z_ps, 1)

            pe.wait_ge(o_s, 1 + UNITS)
            with pe.Fori(0, B - 1, 2) as b:
                output(b, 0)
                output(b, 1)
                back(b, 0)
                back(b, 1)
            ffn(1)


_INS = ['L0_attn_x', 'L0_attn_Wq', 'L0_attn_Wk', 'L0_attn_Wv', 'L0_attn_Wo', 'L0_ffn_router_w',
        'L0_ffn_w1', 'L0_ffn_w2', 'L0_ffn_shared_gate_up', 'L0_ffn_shared_down',
        'L0_ffn_shared_gate_w']


def kernel(**inputs):
    import numpy as _np
    import concourse.bacc as _bacc
    from concourse import mybir as _mybir
    from concourse.bass_utils import run_bass_kernel_spmd as _run

    nc = _bacc.Bacc("TRN2", target_bir_lowering=False, num_devices=1)
    arrays, args = {}, []
    for name in _INS:
        a = _np.ascontiguousarray(inputs[name])
        arrays[f"in_{name}"] = a
        args.append(nc.dram_tensor(f"in_{name}", a.shape, _mybir.dt.from_np(a.dtype),
                                   kind="ExternalInput").ap())
    shape = inputs['L0_attn_x'].shape
    args.append(nc.dram_tensor("out_x", shape, _mybir.dt.float32, kind="ExternalOutput").ap())
    macaron_kernel(nc, *args)
    r = _run(nc, [arrays], core_ids=[0])
    return r.results[0]["out_x"]
```

```python
import concourse.bass as bass
from concourse import mybir
from contextlib import ExitStack


def macaron_kernel(nc, x_in, wq_in, wk_in, wv_in, wo_in, router_in, w1_in, w2_in, gate_up_in,
                   down_in, shared_gate_in, out):
    fp32 = mybir.dt.float32
    fp32r = mybir.dt.float32r
    int32 = mybir.dt.int32
    ALU = mybir.AluOpType
    ACT = mybir.ActivationFunctionType
    AX = mybir.AxisListType
    ds = bass.ds

    B, S, D = x_in.shape
    E, _, F = w1_in.shape
    HD = 64
    H = wq_in.shape[1] // HD
    BLK = 64
    P = 128
    QT = S // P
    NBLK = S // BLK
    PAIRS = H // 2
    UNITS = B * H
    NE = E + 1
    NH = NE + 1
    EPS = 1e-5
    RSQRT_SEED = float(0x5F3759DF)
    FAR = -3.0e38
    TINY = 2.0 ** -60
    TILES = B * QT
    CR = HD + 2 * NBLK

    ctx = ExitStack()
    with ctx:
        def sb(name, shape, dt=fp32):
            return ctx.enter_context(nc.sbuf_tensor(name, shape, dt))

        def sem(name):
            return ctx.enter_context(nc.semaphore(name))

        x = sb("x", [P, TILES * D])
        xT_hi = sb("xT_hi", [D, B * S], fp32r)
        xT_lo = sb("xT_lo", [D, B * S], fp32r)
        w1_hi = sb("w1_hi", [D, NH * F], fp32r)
        w1_lo = sb("w1_lo", [D, NH * F], fp32r)
        w2 = sb("w2", [F, NE * D])
        router_hi = sb("router_hi", [D, P], fp32r)
        router_lo = sb("router_lo", [D, P], fp32r)
        wqkv = sb("wqkv", [D, 3, H * HD])
        wo = sb("wo", [2 * HD, PAIRS * D])
        oT = sb("oT", [2 * HD, B * PAIRS * S])
        w_raw = oT[:, 0:NH * F]
        router_raw = oT[:, 2048:2048 + P]
        sel_raw = oT[:, 4096:4096 + NE * P]
        block_raw = oT[HD:CR, 8192:8192 + S]
        xs_hi = sb("xs_hi", [D, S], fp32r)
        xs_lo = sb("xs_lo", [D, S], fp32r)
        w_hi = sb("w_hi", [D, 3, P], fp32r)
        w_lo = sb("w_lo", [D, 3, P], fp32r)
        qk_pair = sb("qk_pair", [P, 4, S])
        NU = 4
        q_hh = [sb(f"q_hh{n}", [2 * HD, S], fp32r) for n in range(NU)]
        k_hl = [sb(f"k_hl{n}", [2 * HD, S], fp32r) for n in range(NU)]
        q_lc = [sb(f"q_lc{n}", [CR, S], fp32r) for n in range(NU)]
        k_hb = [sb(f"k_hb{n}", [CR, S], fp32r) for n in range(NU)]
        v_st = [sb(f"v_st{n}", [P, QT, P]) for n in range(2)]
        e_sb = sb("e_sb", [P, 2, 2 * S])
        half = sb("half", [P, 2, 2 * NBLK, BLK // 2])
        pT = sb("pT", [P, QT, S])
        hid = e_sb[:, :, :].rearrange("p g (n s) -> p (g n) s", n=2)
        hc = pT
        logitT = pT[0:NE, :, :].rearrange("e b s -> e (b s)")
        xn = half[:, :, :, :].rearrange("p a b c -> p a (b c)")
        comb = xn[:, 0, :].rearrange("p (t e) -> p t e", e=32)
        rt = qk_pair[:, :, :].rearrange("p a (b c) -> p (a b) c", c=TILES * 16)
        ident = sb("ident", [P, P])
        sel = sb("sel", [P, NE * P], fp32r)
        combT = sb("combT", [P, B * S], fp32r)
        stats = sb("stats", [P, TILES, 6])
        rs = sb("rs", [P, 4, TILES])
        ones8 = sb("ones8", [P, TILES * E])
        reset0 = sb("reset0", [P, TILES * NBLK])
        reset1 = sb("reset1", [P, QT * NBLK])
        far0 = sb("far0", [P, QT * NBLK])
        bmax = sb("bmax", [P, 2, QT * NBLK])
        bsum = sb("bsum", [P, QT * NBLK])
        nm = sb("nm", [P, 2, QT])
        st = sb("st", [P, 5, QT * NBLK])
        ctile = sb("ctile", [P, QT, CR])

        psA = ctx.enter_context(nc.psum_tensor("psA", [P, 4, S], fp32))
        psB = [ctx.enter_context(nc.psum_tensor(f"psB{n}", [P, S], fp32)) for n in range(2)]
        psY = ctx.enter_context(nc.psum_tensor("psY", [P, S], fp32))
        psM = ctx.enter_context(nc.psum_tensor("psM", [P, S], fp32))
        cb_banks = (psB[0], psB[1], psM)

        x_in_s = [sem(f"x_in_s{b}") for b in range(B)]; w_in_s = sem("w_in_s"); wa_in_s = sem("wa_in_s")
        r_zero_s = sem("r_zero_s"); r_in_s = sem("r_in_s")
        consts_s = sem("consts_s"); pool_step = sem("pool_step"); split_s = sem("split_s")
        dve_step = sem("dve_step")
        xn_s = sem("xn_s"); xT_ps = sem("xT_ps"); xT_hi_s = sem("xT_hi_s"); xT_lo_s = sem("xT_lo_s")
        logit_ps = sem("logit_ps"); logitT_s = sem("logitT_s"); lt_ps = sem("lt_ps")
        rexp_in = sem("rexp_in"); rexp_s = sem("rexp_s")
        comb_s = sem("comb_s"); combT_ps = sem("combT_ps"); combT_s = sem("combT_s")
        hid_ps = sem("hid_ps"); silu_s = sem("silu_s"); up_s = sem("up_s")
        cb_ps = sem("cb_ps"); hc_s = sem("hc_s"); y_ps = sem("y_ps"); x_s = sem("x_s")
        xs_s = sem("xs_s"); wqk_s = sem("wqk_s"); wv_s = sem("wv_s")
        q_ps = sem("q_ps"); q_hi_s = sem("q_hi_s"); q_lo_s = sem("q_lo_s")
        k_ps = sem("k_ps"); k_hi_s = sem("k_hi_s"); k_lo_s = sem("k_lo_s")
        v_ps = sem("v_ps"); v_s = sem("v_s"); qk0_s = sem("qk0_s"); qk1_s = sem("qk1_s")
        s_ps = sem("s_ps"); nm_s = sem("nm_s"); e_s = sem("e_s"); half_s = sem("half_s")
        bsum_s = sem("bsum_s"); ln_in = sem("ln_in"); ln_s = sem("ln_s")
        c_s = sem("c_s"); cT_ps = sem("cT_ps"); cT_s = sem("cT_s")
        sT_ps = sem("sT_ps"); pT_s = sem("pT_s"); o_ps = sem("o_ps"); o_s = sem("o_s")
        zT_ps = sem("zT_ps"); zT_s = sem("zT_s"); z_ps = sem("z_ps"); z_s = sem("z_s")
        out_s = sem("out_s")

        block = ctx.enter_context(nc.Block())

        QK_DMAS = 6
        FFN_LAG = 2

        def raw(ap):
            return ap.bitcast(fp32)

        def past(eng, semaphore, count):
            if not isinstance(count, int) or count > 0:
                eng.wait_ge(semaphore, count)

        TURNS = UNITS // NU

        def in_slots(eng, slot):
            for i in (-1, 0):
                for s in range(NU):
                    slot(i, s)
            with eng.Fori(1, TURNS - 1) as i:
                for s in range(NU):
                    slot(i, s)
            for s in range(NU):
                slot(TURNS - 1, s)

        def unit(i, k):
            return i * NU + k

        def pair(i, k):
            return i * (NU // 2) + k // 2

        def is_unit(u):
            return not isinstance(u, int) or 0 <= u < UNITS

        def is_pair(p):
            return not isinstance(p, int) or 0 <= p < UNITS // 2

        @block.sync
        def _(sp):
            xv = x[:, :].rearrange("p (t d) -> p t d", d=D)
            for b in range(B):
                sp.dma_start(xv[:, b * QT:(b + 1) * QT, :],
                             x_in[b].rearrange("(t p) d -> p t d", p=P)).then_inc(x_in_s[b], 16)
            for n, w in enumerate((wq_in, wk_in, wv_in)):
                sp.dma_start(wqkv[:, n, :], w).then_inc(wa_in_s, 16)
            sp.dma_start(wo[:, :].rearrange("r (h d) -> r h d", d=D),
                         wo_in.rearrange("(h r) d -> r h d", r=2 * HD)).then_inc(wa_in_s, 16)

            def head_copies(n, h, p, done):
                rows = slice(h * HD, (h + 1) * HD)
                for to in range(2):
                    sp.dma_start(raw(q_hh[n][to * HD:(to + 1) * HD, :]), qk_pair[rows, 0, :])\
                      .then_inc(done, 16)
                sp.dma_start(raw(q_lc[n][0:HD, :]), qk_pair[rows, 1, :]).then_inc(done, 16)
                sp.dma_start(raw(k_hl[n][0:HD, :]), qk_pair[rows, 2, :]).then_inc(done, 16)
                sp.dma_start(raw(k_hb[n][0:HD, :]), qk_pair[rows, 2, :]).then_inc(done, 16)
                sp.dma_start(raw(k_hl[n][HD:2 * HD, :]), qk_pair[rows, 3, :]).then_inc(done, 16)

            def load_xs(b):
                sp.wait_ge(xT_hi_s, B + 1 + b)
                sp.wait_ge(xT_lo_s, B + 1 + b)
                sp.dma_start(raw(xs_hi[:, :]), raw(xT_hi[:, ds(b * S, S)])).then_inc(xs_s, 16)
                sp.dma_start(raw(xs_lo[:, :]), raw(xT_lo[:, ds(b * S, S)])).then_inc(xs_s, 16)

            def slot(i, s):
                u, p = unit(i, s), pair(i, s + NU)
                if s == 2 and is_pair(pair(i, s + 2)) and not (isinstance(i, int) and i < 0):
                    sp.wait_ge(v_ps, pair(i, s + 2))
                    load_xs(unit(i, s + 2) // H)
                if is_pair(p):
                    if s % 2 == 0:
                        sp.wait_ge(k_lo_s, p + 1)
                    else:
                        past(sp, sT_ps, QT * (u + 1))
                    head_copies(s, s % 2, p, (qk0_s, qk1_s)[s % 2])

            load_xs(0)
            in_slots(sp, slot)
            for b in range(B):
                sp.wait_ge(x_s, B + b + 1)
                sp.dma_start(out[b].rearrange("(t p) d -> p t d", p=P),
                             xv[:, b * QT:(b + 1) * QT, :]).then_inc(out_s, 16)
            sp.wait_ge(out_s, 16 * B)

        @block.gpsimd
        def _(pool):
            steps = [0]

            def step(ins):
                steps[0] += 1
                ins.then_inc(pool_step, 1)
                pool.wait_ge(pool_step, steps[0])

            pool.memset(router_raw, 0.0).then_inc(r_zero_s, 1)
            pool.wait_ge(r_zero_s, 1)
            for tile, value in ((ident[:, :], 0.0), (sel_raw, 0.0), (reset0[:, :], 1.0),
                                (reset1[:, :], 1.0), (ones8[:, :], 1.0), (far0[:, :], 0.0),
                                (raw(combT[:, :]), 0.0), (ctile[:, :, :], 0.0), (block_raw, 0.0)):
                step(pool.memset(tile, value))
            step(pool.affine_select(out=ident[:, :], in_=ident[:, :], compare_op=ALU.not_equal, fill=1.0,
                                    base=0, pattern=[[-1, P]], channel_multiplier=1))
            selv = sel_raw[0:2 * NE, :].rearrange("r (e f) -> r e f", f=P)
            for twin in range(2):
                step(pool.affine_select(out=selv, in_=selv, compare_op=ALU.not_equal, fill=1.0,
                                        base=twin * NE, pattern=[[1, NE], [0, P]],
                                        channel_multiplier=-1))
            blv = block_raw.rearrange("r (j k) -> r j k", k=BLK)
            for twin in range(2):
                step(pool.affine_select(out=blv, in_=blv, compare_op=ALU.not_equal, fill=1.0,
                                        base=twin * NBLK, pattern=[[1, NBLK], [0, BLK]],
                                        channel_multiplier=-1))
            for tile, at, value in ((reset0, 0, 0.0), (reset1, NBLK - 1, 0.0), (far0, 0, FAR)):
                tv = tile[:, :].rearrange("p (t j) -> p t j", j=NBLK)
                step(pool.memset(tv[:, :, at:at + 1], value))
            pool.tensor_copy(sel[:, :], sel_raw).then_inc(consts_s, 1)
            pool.wait_ge(consts_s, 1)
            for n in range(NU):
                pool.tensor_copy(k_hb[n][HD:CR, :], block_raw).then_inc(consts_s, 1)
                pool.wait_ge(consts_s, n + 2)

            def split_hi(p, which, used, done):
                past(pool, used, p)
                src = wqkv[:, which, ds((p % PAIRS) * P, P)]
                pool.tensor_copy(w_hi[:, which, :], src).then_inc(done, 1)
                pool.wait_ge(done, 2 * p + 1)
                return src

            def split_lo(src, which, done):
                pool.tensor_tensor(w_lo[:, which, :], src, raw(w_hi[:, which, :]), ALU.subtract)\
                    .then_inc(done, 1)

            QK, VV = slice(0, 2), slice(2, 3)

            def slot(i, s):
                n = unit(i, s + 2)
                if s % 2 == 1:
                    which, used, done, p = QK, k_ps, wqk_s, pair(i, s + 5)
                else:
                    which, used, done, p = VV, v_ps, wv_s, pair(i, s + 2)
                if is_pair(p):
                    src = split_hi(p, which, used, done)
                for g in range(2):
                    if is_unit(n):
                        pool.wait_ge(e_s, 2 * n + g + 1)
                        past(pool, bsum_s, 2 * n + g - 1)
                        ev = e_sb[:, g, :].rearrange("p (j k) -> p j k", k=BLK)
                        pool.tensor_tensor(half[:, g, :, :], ev[:, :, 0:BLK // 2],
                                           ev[:, :, BLK // 2:BLK], ALU.add).then_inc(half_s, 1)
                    if g == 0 and is_pair(p):
                        split_lo(src, which, done)

            pool.wait_ge(wa_in_s, 16 * 4)
            src = split_hi(0, QK, k_ps, wqk_s)
            split_lo(src, QK, wqk_s)
            in_slots(pool, slot)

        @block.scalar
        def _(act):
            act.wait_ge(r_zero_s, 1)
            act.dma_start(router_raw[:, 0:E], router_in).then_inc(r_in_s, 16)
            act.dma_start(router_raw[:, E:NE], shared_gate_in).then_inc(r_in_s, 16)
            act.dma_start(w_raw[:, 0:E * F].rearrange("d (e f) -> d e f", f=F),
                          w1_in.rearrange("e d f -> d e f")).then_inc(w_in_s, 16)
            act.dma_start(w_raw[:, E * F:NH * F], gate_up_in).then_inc(w_in_s, 16)
            act.dma_start(w2[:, 0:E * D].rearrange("f (e d) -> f e d", d=D),
                          w2_in.rearrange("e f d -> f e d")).then_inc(w_in_s, 16)
            act.dma_start(w2[:, E * D:NE * D], down_in).then_inc(w_in_s, 16)

            def turned(norm):
                for b in range(B):
                    act.wait_ge(xT_ps, B * norm + b + 1)
                    nc.scalar.activation(xT_hi[:, b * S:(b + 1) * S], psA[:, b, :], ACT.Copy)\
                        .then_inc(xT_hi_s, 1)

            def ffn(phase):
                turned(2 * phase)
                for b in range(B):
                    act.wait_ge(logit_ps, B * phase + b + 1)
                    nc.scalar.activation(logitT[:, b * S:(b + 1) * S], psB[b % 2][0:NE, :], ACT.Copy)\
                        .then_inc(logitT_s, 1)
                act.wait_ge(rexp_in, phase + 1)
                lv = rt[:, 1, :].rearrange("p (t e) -> p t e", e=16)
                nc.scalar.activation(lv[:, :, 0:E], lv[:, :, 0:E], ACT.Exp).then_inc(rexp_s, 1)
                nc.scalar.activation(lv[:, :, E:NE], lv[:, :, E:NE], ACT.Tanh, scale=0.5)\
                    .then_inc(rexp_s, 1)

                def silu(b, e):
                    g = b + B * phase
                    act.wait_ge(hid_ps, NH * g + e + 1)
                    past(act, hc_s, NE * g + e - 2)
                    nc.scalar.activation(hid[:, e % 3, :], psA[:, e % 4, :], ACT.Silu)\
                        .then_inc(silu_s, 1)

                def experts(b, first):
                    for e in range(NE):
                        silu(b, e)
                        if first and e == 0:
                            for k in range(B):
                                act.wait_ge(combT_ps, B * phase + k + 1)
                                nc.scalar.activation(combT[0:2 * NE, k * S:(k + 1) * S],
                                                     (psM, psY)[k % 2][0:2 * NE, :], ACT.Copy)\
                                    .then_inc(combT_s, 1)

                experts(0, True)
                with act.Fori(1, B) as b:
                    experts(b, False)

            act.wait_ge(w_in_s, 16 * 4)
            act.wait_ge(r_in_s, 32)
            nc.scalar.activation(router_hi[:, :], router_raw, ACT.Copy).then_inc(split_s, 1)
            nc.scalar.activation(w1_hi[:, :], w_raw, ACT.Copy).then_inc(split_s, 1)
            ffn(0)
            turned(1)
            act.preload_act_table_set("natural_log_exp_and_others")

            def output(u, s):
                rows = slice((s % 2) * HD, (s % 2 + 1) * HD)
                act.wait_ge(o_ps, u + 1)
                nc.scalar.activation(oT[rows, ds((u // 2) * S, S)], psY[rows, :], ACT.Copy)\
                    .then_inc(o_s, 1)

            def slot(i, s):
                u, m, n = unit(i, s), unit(i, s + 1), unit(i, s + 2)

                def exps(g):
                    if is_unit(n):
                        act.wait_ge(nm_s, 2 * n + g + 1)
                        past(act, half_s, 2 * n + g - 1)
                        for q in (2 * g, 2 * g + 1):
                            ins = nc.scalar.activation(e_sb[:, g, (q % 2) * S:(q % 2 + 1) * S],
                                                       psA[:, q, :], ACT.Exp,
                                                       bias=nm[:, s % 2, q:q + 1])
                        ins.then_inc(e_s, 1)

                def weighted(k):
                    if is_unit(u):
                        act.wait_ge(sT_ps, QT * u + k + 1)
                        nc.scalar.activation(pT[:, k, :], psB[k % 2][:, :], ACT.Exp).then_inc(pT_s, 1)

                weighted(0)
                weighted(1)
                if is_unit(unit(i, s - 1)):
                    output(unit(i, s - 1), s - 1)
                p, pv = pair(i, s + 4), pair(i, s + 1)
                qk = s % 2 == 0 and is_pair(p)
                if qk:
                    act.wait_ge(q_ps, p + 1)
                    past(act, qk0_s, 16 * QK_DMAS * p)
                    past(act, qk1_s, 16 * QK_DMAS * p)
                    nc.scalar.activation(qk_pair[:, 0, :].bitcast(fp32r), psM[:, :], ACT.Copy,
                                         scale=HD ** -0.5).then_inc(q_hi_s, 1)
                if s % 2 == 1 and is_pair(pv):
                    act.wait_ge(v_ps, pv + 1)
                    nc.scalar.activation(v_st[(s // 2 + 1) % 2][:, :, :].rearrange("p t d -> p (t d)"),
                                         psM[:, :], ACT.Copy).then_inc(v_s, 1)
                exps(0)
                if is_unit(m):
                    act.wait_ge(ln_in, m + 1)
                    nc.scalar.activation(st[:, 2, :], st[:, 2, :], ACT.Ln).then_inc(ln_s, 1)
                weighted(2)
                weighted(3)
                if is_unit(m):
                    act.wait_ge(cT_ps, m + 1)
                    nc.scalar.activation(q_lc[(s + 1) % NU][HD:CR, :], psA[HD:CR, 0, :], ACT.Copy)\
                        .then_inc(cT_s, 1)
                exps(1)
                if qk:
                    act.wait_ge(k_ps, p + 1)
                    nc.scalar.activation(qk_pair[:, 2, :].bitcast(fp32r), psM[:, :], ACT.Copy)\
                        .then_inc(k_hi_s, 1)

            in_slots(act, slot)
            output(UNITS - 1, UNITS - 1)

            for b in range(B):
                act.wait_ge(zT_ps, b + 1)
                nc.scalar.activation(pT[:, b, :], psA[:, b, :], ACT.Copy).then_inc(zT_s, 1)
            ffn(1)

        @block.vector
        def _(dve):
            V = nc.vector
            base, at, turn = [0], [0], [None, 0]

            def post(ins):
                at[0] += 1
                ins.then_inc(dve_step, 1)
                return at[0]

            def need(mark):
                dve.wait_ge(dve_step, base[0] + mark if turn[0] is None
                            else turn[0] * turn[1] + (base[0] + mark))

            def step(ins):
                need(post(ins))

            def norm(phase, ready):
                for b in range(B):
                    ready(b)
                    for t in range(QT * b, QT * (b + 1)):
                        ins = V.bn_stats(stats[:, t, :], x[:, t * D:(t + 1) * D])
                step(ins)
                me, qe, mo, qo = (stats[:, :, k] for k in (1, 2, 4, 5))
                mean, var, y, a = (rs[:, k, :] for k in range(4))
                V.tensor_tensor(a, me, mo, ALU.subtract)
                V.tensor_tensor(mean, me, mo, ALU.add)
                step(V.tensor_tensor(var, qe, qo, ALU.add))
                V.scalar_tensor_tensor(a, a, 0.25, a, ALU.mult, ALU.mult)
                V.tensor_scalar(mean, mean, 0.5, None, ALU.mult)
                step(V.tensor_scalar(var, var, 1.0 / D, EPS, ALU.mult, ALU.add))
                step(V.tensor_tensor(var, var, a, ALU.add))
                step(V.tensor_scalar(y.bitcast(int32), var.bitcast(int32), -0.5, RSQRT_SEED,
                                     ALU.mult, ALU.add))
                for _ in range(3):
                    step(V.scalar_tensor_tensor(a, y, -0.5, var, ALU.mult, ALU.mult))
                    step(V.tensor_tensor(a, a, y, ALU.mult))
                    step(V.scalar_tensor_tensor(y, a, 1.5, y, ALU.add, ALU.mult))

                def lo(b):
                    dve.wait_ge(xT_hi_s, B * phase + b + 1)
                    V.tensor_tensor(xT_lo[:, b * S:(b + 1) * S], psA[:, b, :],
                                    raw(xT_hi[:, b * S:(b + 1) * S]), ALU.subtract)\
                     .then_inc(xT_lo_s, 1)

                for b in range(B):
                    if b >= 2:
                        dve.wait_ge(xT_ps, B * phase + b - 1)
                    for t in range(QT):
                        k = QT * b + t
                        ins = V.tensor_scalar(xn[:, b % 2, t * D:(t + 1) * D], x[:, k * D:(k + 1) * D],
                                              mean[:, k:k + 1], y[:, k:k + 1], ALU.subtract, ALU.mult)
                    ins.then_inc(xn_s, 1)
                    if b >= 1:
                        lo(b - 1)
                lo(B - 1)

            def router(phase):
                logit, ls, m, pc, sel1, sel2, w = (rt[:, n, :].rearrange("p (t e) -> p t e", e=16)
                                                   for n in range(7))
                flat = rt[:, 7, :]
                mask_f, count_f = flat[:, 0:TILES * E], flat[:, TILES * E:2 * TILES * E]
                mask = mask_f.rearrange("p (t e) -> p t e", e=E)
                count = count_f.rearrange("p (t e) -> p t e", e=E)

                def over_e(v):
                    return v.broadcast_to([P, TILES, E])

                dve.wait_ge(lt_ps, phase + 1)
                step(V.tensor_copy(logit[:, :, 0:NE],
                                   psM[:, 0:TILES * 16].rearrange("p (t e) -> p t e", e=16)[:, :, 0:NE]))
                step(V.tensor_reduce(m[:, :, 8:9], logit[:, :, 0:E], AX.X, ALU.max))
                V.tensor_copy(ls[:, :, E:NE], logit[:, :, E:NE])
                V.tensor_tensor(ls[:, :, 0:E], logit[:, :, 0:E], over_e(m[:, :, 8:9]), ALU.subtract)\
                 .then_inc(rexp_in, 1)
                step(V.tensor_tensor(w[:, :, 0:E], logit[:, :, 0:E], over_e(m[:, :, 8:9]), ALU.subtract))

                def first_of(dst):
                    step(V.tensor_tensor_scan(count_f, reset0[:, 0:TILES * E], mask_f, 0.0,
                                              ALU.mult, ALU.add))
                    step(V.scalar_tensor_tensor(dst[:, :, 0:E], count, 1.0, mask,
                                                ALU.is_equal, ALU.mult))

                step(V.tensor_scalar(mask, w[:, :, 0:E], 0.0, None, ALU.is_equal))
                first_of(sel1)
                step(V.scalar_tensor_tensor(w[:, :, 0:E], sel1[:, :, 0:E], FAR, w[:, :, 0:E],
                                            ALU.mult, ALU.add))
                step(V.tensor_reduce(m[:, :, 8:9], w[:, :, 0:E], AX.X, ALU.max))
                step(V.tensor_tensor(mask, w[:, :, 0:E], over_e(m[:, :, 8:9]), ALU.is_equal))
                first_of(sel2)
                step(V.tensor_tensor(sel1[:, :, 0:E], sel1[:, :, 0:E], sel2[:, :, 0:E], ALU.add))
                dve.wait_ge(rexp_s, 2 * phase + 2)
                step(V.tensor_reduce(m[:, :, 9:10], ls[:, :, 0:E], AX.X, ALU.add))
                step(V.reciprocal(m[:, :, 10:11], m[:, :, 9:10]))
                step(V.scalar_tensor_tensor(w[:, :, 0:E], ls[:, :, 0:E], 0.5, sel1[:, :, 0:E],
                                            ALU.mult, ALU.mult))
                V.tensor_tensor(w[:, :, 0:E], w[:, :, 0:E], over_e(m[:, :, 10:11]), ALU.mult)
                step(V.tensor_scalar(w[:, :, E:NE], ls[:, :, E:NE], 0.25, 0.25, ALU.mult, ALU.add))
                step(V.tensor_copy(comb[:, :, 0:NE].bitcast(fp32r), w[:, :, 0:NE]))
                V.tensor_tensor(comb[:, :, NE:2 * NE], w[:, :, 0:NE], comb[:, :, 0:NE],
                                ALU.subtract).then_inc(comb_s, 1)

            def ffn(phase, ready):
                def weigh(b, e):
                    g = b + B * phase
                    dve.wait_ge(silu_s, NE * g + e + 1)
                    src = hid[:, e % 3, :]
                    if e == NE - 1:
                        dve.wait_ge(hid_ps, NH * g + NH)
                        past(dve, hc_s, NE * g)
                        V.tensor_tensor(hid[:, 3, :], src, psA[:, (e + 1) % 4, :], ALU.mult)\
                         .then_inc(up_s, 1)
                        dve.wait_ge(up_s, g + 1)
                        src = hid[:, 3, :]
                    dve.wait_ge(cb_ps, NE * g + e + 1)
                    past(dve, y_ps, NE * g + e - 2)
                    V.tensor_tensor(hc[:, e % 3, :], src, cb_banks[e % 3][:, :], ALU.mult).then_inc(hc_s, 1)

                def add(b):
                    g = b + B * phase
                    dve.wait_ge(y_ps, NE * (g + 1))
                    xb = x[:, ds(b * (QT * D), QT * D)]
                    V.tensor_tensor(xb, xb, psY[:, :], ALU.add).then_inc(x_s, 1)

                norm(2 * phase, ready)
                router(phase)
                for e in range(NE):
                    weigh(0, e)
                with dve.Fori(1, B) as b:
                    for e in range(NE):
                        weigh(b, e)
                        if e == FFN_LAG - 1:
                            add(b - 1)
                add(B - 1)

            step(V.memset(rt[:, :, :], 0.0))
            dve.wait_ge(split_s, 2)
            V.tensor_tensor(router_lo[:, :], router_raw, raw(router_hi[:, :]), ALU.subtract)
            V.tensor_tensor(w1_lo[:, :], w_raw, raw(w1_hi[:, :]), ALU.subtract).then_inc(split_s, 1)
            ffn(0, lambda b: dve.wait_ge(x_in_s[b], 16))
            norm(1, lambda b: dve.wait_ge(x_s, b + 1))

            def tiles(ap):
                return ap.rearrange("p (t j) -> p t j", j=NBLK)

            def each(ap):
                return ap.rearrange("p (t o) -> p t o", o=1).broadcast_to([P, QT, NBLK])

            def slot(i, s):
                m, n = unit(i, s + 1), unit(i, s + 2)
                p = pair(i, s + 4)
                qk = s % 2 == 0 and is_pair(p)
                pm, dd, lsum, back, c = (st[:, k, :] for k in range(5))
                bmax_m, nm_m = bmax[:, (s + 1) % 2, :], nm[:, (s + 1) % 2, :]
                bmax_n, nm_n = bmax[:, s % 2, :], nm[:, s % 2, :]

                def sums(g):
                    dve.wait_ge(half_s, 2 * m + g + 1)
                    V.tensor_reduce(bsum[:, g * 2 * NBLK:(g + 1) * 2 * NBLK], half[:, g, :, :],
                                    AX.X, ALU.add).then_inc(bsum_s, 1)

                def maxima(g):
                    dve.wait_ge(s_ps, 2 * n + g + 1)
                    return post(V.tensor_reduce(
                        bmax_n[:, g * 2 * NBLK:(g + 1) * 2 * NBLK],
                        psA[:, 2 * g:2 * g + 2, :].rearrange("p t (j k) -> p (t j) k", k=BLK),
                        AX.X, ALU.max))

                def negated(g, mark):
                    need(mark)
                    V.tensor_reduce(nm_n[:, 2 * g:2 * g + 2], tiles(bmax_n)[:, 2 * g:2 * g + 2, :],
                                    AX.X, ALU.max, negate=True).then_inc(nm_s, 1)

                if is_unit(m):
                    sums(0)
                    m1 = post(V.tensor_tensor_scan(pm, far0[:, :], bmax_m, FAR, ALU.add, ALU.max))
                if is_unit(n):
                    m3 = maxima(0)
                if is_unit(m):
                    need(m1)
                    m2 = post(V.tensor_tensor(tiles(dd), tiles(pm), each(nm_m), ALU.add))
                if is_unit(n):
                    negated(0, m3)
                if is_unit(m):
                    sums(1)
                    dve.wait_ge(bsum_s, 2 * m + 2)
                    step(V.tensor_tensor_scan(lsum, reset0[:, 0:QT * NBLK], bsum[:, :], 0.0,
                                              ALU.mult, ALU.add))
                    V.tensor_scalar(lsum, lsum, TINY, None, ALU.max).then_inc(ln_in, 1)
                if qk:
                    dve.wait_ge(q_hi_s, p + 1)
                    V.scalar_tensor_tensor(qk_pair[:, 1, :].bitcast(fp32r), psM[:, :], HD ** -0.5,
                                           qk_pair[:, 0, :], ALU.mult, ALU.subtract)\
                     .then_inc(q_lo_s, 1)
                if is_unit(m):
                    dve.wait_ge(ln_s, m + 1)
                    need(m2)
                    step(V.tensor_tensor(lsum, lsum, dd, ALU.subtract))
                    step(V.tensor_tensor_scan(back[:, ::-1], reset1[:, ::-1], lsum[:, ::-1], 0.0,
                                              ALU.mult, ALU.add))
                    step(V.tensor_tensor(tiles(c), each(nm_m), tiles(back), ALU.subtract))
                    step(V.tensor_copy(ctile[:, :, HD:HD + NBLK].bitcast(fp32r), tiles(c)))
                    V.tensor_tensor(ctile[:, :, HD + NBLK:CR], tiles(c), ctile[:, :, HD:HD + NBLK],
                                    ALU.subtract).then_inc(c_s, 1)
                if is_unit(n):
                    m4 = maxima(1)
                    negated(1, m4)
                if qk:
                    dve.wait_ge(k_hi_s, p + 1)
                    V.tensor_tensor(qk_pair[:, 3, :].bitcast(fp32r), psM[:, :], qk_pair[:, 2, :],
                                    ALU.subtract).then_inc(k_lo_s, 1)

            SLOT_MARKS = 9
            for i in (-1, 0):
                for s in range(NU):
                    slot(i, s)
            base[0] += at[0] - NU * SLOT_MARKS
            at[0] = 0
            with dve.Fori(1, TURNS - 1) as i:
                turn[:] = [i, NU * SLOT_MARKS]
                for s in range(NU):
                    slot(i, s)
            assert at[0] == NU * SLOT_MARKS, at[0]
            turn[0] = None
            base[0] += NU * SLOT_MARKS * (TURNS - 1)
            at[0] = 0
            for s in range(NU):
                slot(TURNS - 1, s)

            for b in range(B):
                dve.wait_ge(z_ps, b + 1)
                xb = x[:, b * (QT * D):(b + 1) * (QT * D)]
                V.tensor_tensor(xb, xb, psB[b % 2][:, :], ALU.add).then_inc(z_s, 1)
            ffn(1, lambda b: dve.wait_ge(z_s, b + 1))

        @block.tensor
        def _(pe):
            T = nc.tensor

            def three(o, w_hi_, w_lo_, r_hi, r_lo):
                T.matmul(o, w_hi_, r_hi, start=True, stop=False)
                T.matmul(o, w_hi_, r_lo, start=False, stop=False)
                return T.matmul(o, w_lo_, r_hi, start=False, stop=True)

            def turn_x(norm):
                for b in range(B):
                    pe.wait_ge(xn_s, B * norm + b + 1)
                    for t in range(QT):
                        ins = T.transpose(psA[:, b, t * P:(t + 1) * P], xn[:, b % 2, t * D:(t + 1) * D],
                                          ident[:, :])
                    ins.then_inc(xT_ps, 1)

            def ffn(phase):
                def hidden(b, j):
                    g = b + B * phase
                    if j >= 4:
                        pe.wait_ge(silu_s, NE * g + j - 3)
                    elif j == 1:
                        past(pe, up_s, g)
                    else:
                        past(pe, silu_s, NE * g)
                    three(psA[:, j % 4, :], w1_hi[:, j * F:(j + 1) * F], w1_lo[:, j * F:(j + 1) * F],
                          xT_hi[:, ds(b * S, S)], xT_lo[:, ds(b * S, S)]).then_inc(hid_ps, 1)

                def combine(b, e):
                    g = b + B * phase
                    past(pe, hc_s, NE * g + e - 2)
                    T.matmul(cb_banks[e % 3][:, :], sel[:, e * P:(e + 1) * P],
                             combT[:, ds(b * S, S)], start=True, stop=True).then_inc(cb_ps, 1)

                def second(b, e):
                    g = b + B * phase
                    pe.wait_ge(hc_s, NE * g + e + 1)
                    if e == 0:
                        past(pe, x_s, g)
                    for t in range(QT):
                        ins = T.matmul(psY[:, t * D:(t + 1) * D], hc[:, e % 3, t * P:(t + 1) * P],
                                       w2[:, e * D:(e + 1) * D], start=(e == 0 and t == 0),
                                       stop=(e == NE - 1 and t == QT - 1), skip_group_check=True)
                    ins.then_inc(y_ps, 1)

                def experts(b, first):
                    for e in range(NE):
                        if not (first and e < 4):
                            hidden(b, e)
                        if e == NE - 1:
                            hidden(b, NE)
                        combine(b, e)
                        if e >= FFN_LAG:
                            second(b, e - FFN_LAG)
                        elif not first:
                            second(b - 1, NE + e - FFN_LAG)

                turn_x(2 * phase)
                if phase == 0:
                    pe.wait_ge(split_s, 3)
                for b in range(B):
                    pe.wait_ge(xT_lo_s, 2 * B * phase + b + 1)
                    if b >= 2:
                        pe.wait_ge(logitT_s, B * phase + b - 1)
                    three(psB[b % 2][:, :], router_hi[:, :], router_lo[:, :],
                          xT_hi[:, b * S:(b + 1) * S], xT_lo[:, b * S:(b + 1) * S]).then_inc(logit_ps, 1)
                pe.wait_ge(logitT_s, B * (phase + 1))
                for t in range(TILES):
                    ins = T.transpose(psM[:, t * 16:t * 16 + NE], logitT[:, t * P:(t + 1) * P],
                                      ident[0:NE, 0:NE])
                ins.then_inc(lt_ps, 1)
                if phase == 0:
                    pe.wait_ge(w_in_s, 16 * 4)
                for j in range(4):
                    hidden(0, j)
                pe.wait_ge(comb_s, phase + 1)
                for b in range(B):
                    if b >= 2:
                        pe.wait_ge(combT_s, B * phase + b - 1)
                    for t in range(QT):
                        ins = T.transpose((psM, psY)[b % 2][0:2 * NE, t * P:(t + 1) * P],
                                          comb[:, b * QT + t, 0:2 * NE], ident[:, :])
                    ins.then_inc(combT_ps, 1)
                pe.wait_ge(combT_s, B * (phase + 1))
                experts(0, True)
                with pe.Fori(1, B) as b:
                    experts(b, False)
                for e in range(NE - FFN_LAG, NE):
                    second(B - 1, e)

            pe.wait_ge(consts_s, 1 + NU)
            ffn(0)
            turn_x(1)

            def slot(i, s):
                u, m, n = unit(i, s), unit(i, s + 1), unit(i, s + 2)
                tn, tu = (s + 2) % NU, s % NU

                def scores(g):
                    if not is_unit(n):
                        return
                    if g == 0:
                        pe.wait_ge((qk0_s, qk1_s)[s % 2], 16 * QK_DMAS * (pair(i, s + 2) + 1))
                    past(pe, e_s, 2 * n + g - 1)
                    for q in (2 * g, 2 * g + 1):
                        T.matmul(psA[:, q, :], q_hh[tn][:, q * P:(q + 1) * P], k_hl[tn][:, :],
                                 start=True, stop=False)
                    for q in (2 * g, 2 * g + 1):
                        ins = T.matmul(psA[:, q, :], q_lc[tn][0:HD, q * P:(q + 1) * P],
                                       k_hl[tn][0:HD, :], start=False, stop=True)
                    ins.then_inc(s_ps, 1)

                def scoresT(ks):
                    if not is_unit(u):
                        return
                    for k in ks:
                        T.matmul(psB[k % 2][:, :], k_hl[tu][:, k * P:(k + 1) * P], q_hh[tu][:, :],
                                 start=True, stop=False)
                    if ks[0] == 0:
                        pe.wait_ge(cT_s, u + 1)
                    for k in ks:
                        T.matmul(psB[k % 2][:, :], k_hb[tu][:, k * P:(k + 1) * P], q_lc[tu][:, :],
                                 start=False, stop=True).then_inc(sT_ps, 1)

                def pv(k):
                    if not is_unit(u):
                        return
                    rows = slice((s % 2) * HD, (s % 2 + 1) * HD)
                    if k == 0:
                        pe.wait_ge(v_s, pair(i, s) + 1)
                        past(pe, o_s, u - 1)
                    pe.wait_ge(pT_s, QT * u + k + 1)
                    ins = T.matmul(psY[rows, :], v_st[s // 2][:, k, rows], pT[:, k, :],
                                   start=(k == 0), stop=(k == QT - 1))
                    if k == QT - 1:
                        ins.then_inc(o_ps, 1)

                p, pv_pair = pair(i, s + 4), pair(i, s + 1)
                qk = s % 2 == 0 and is_pair(p)

                def project(which, done):
                    at = ds((p // PAIRS) * S, S)
                    three(psM[:, :], w_hi[:, which, :], w_lo[:, which, :], xT_hi[:, at], xT_lo[:, at])\
                        .then_inc(done, 1)

                scoresT((0, 1))
                scores(0)
                if qk:
                    pe.wait_ge(wqk_s, 2 * p + 2)
                    past(pe, v_s, pair(i, s))
                    project(0, q_ps)
                if s % 2 == 1 and is_pair(pv_pair):
                    pe.wait_ge(wv_s, 2 * pv_pair + 2)
                    pe.wait_ge(xs_s, 32 * (i + (s + 1) // 2))
                    if is_pair(pair(i, s + 3)):
                        pe.wait_ge(k_lo_s, pair(i, s + 3) + 1)
                    for t in range(QT):
                        tt = slice(t * P, (t + 1) * P)
                        ins = three(psM[:, tt], xs_hi[:, tt], xs_lo[:, tt], w_hi[:, 2, :], w_lo[:, 2, :])
                    ins.then_inc(v_ps, 1)
                pv(0)
                scoresT((2,))
                pv(1)
                scores(1)
                scoresT((3,))
                pv(2)
                if is_unit(m):
                    pe.wait_ge(c_s, m + 1)
                    if is_unit(n):
                        pe.wait_ge(e_s, 2 * n + 1)
                    for q in range(QT):
                        ins = T.transpose(psA[0:CR, 0, q * P:(q + 1) * P], ctile[:, q, :], ident[:, :])
                    ins.then_inc(cT_ps, 1)
                if qk:
                    pe.wait_ge(q_hi_s, p + 1)
                    pe.wait_ge(q_lo_s, p + 1)
                    project(1, k_ps)
                pv(3)

            for b in range(B):
                pe.wait_ge(xT_lo_s, B + b + 1)
            in_slots(pe, slot)

            def turn_back(b):
                pe.wait_ge(zT_s, b + 1)
                if b >= 2:
                    pe.wait_ge(z_s, b - 1)
                for t in range(QT):
                    ins = T.transpose(psB[b % 2][:, t * P:(t + 1) * P], pT[:, b, t * P:(t + 1) * P],
                                      ident[:, :])
                ins.then_inc(z_ps, 1)

            for b in range(B):
                pe.wait_ge(o_s, H * (b + 1))
                for h in range(PAIRS):
                    ins = T.matmul(psA[:, b, :], wo[:, h * D:(h + 1) * D],
                                   oT[:, (b * PAIRS + h) * S:(b * PAIRS + h + 1) * S],
                                   start=(h == 0), stop=(h == PAIRS - 1))
                ins.then_inc(zT_ps, 1)
                if b >= 1:
                    turn_back(b - 1)
            turn_back(B - 1)
            ffn(1)


_INS = ['L0_attn_x', 'L0_attn_Wq', 'L0_attn_Wk', 'L0_attn_Wv', 'L0_attn_Wo', 'L0_ffn_router_w',
        'L0_ffn_w1', 'L0_ffn_w2', 'L0_ffn_shared_gate_up', 'L0_ffn_shared_down',
        'L0_ffn_shared_gate_w']


def kernel(**inputs):
    import numpy as _np
    import concourse.bacc as _bacc
    from concourse import mybir as _mybir
    from concourse.bass_utils import run_bass_kernel_spmd as _run

    nc = _bacc.Bacc("TRN2", target_bir_lowering=False, num_devices=1)
    arrays, args = {}, []
    for name in _INS:
        a = _np.ascontiguousarray(inputs[name])
        arrays[f"in_{name}"] = a
        args.append(nc.dram_tensor(f"in_{name}", a.shape, _mybir.dt.from_np(a.dtype),
                                   kind="ExternalInput").ap())
    shape = inputs['L0_attn_x'].shape
    args.append(nc.dram_tensor("out_x", shape, _mybir.dt.float32, kind="ExternalOutput").ap())
    macaron_kernel(nc, *args)
    r = _run(nc, [arrays], core_ids=[0])
    return r.results[0]["out_x"]
```

```python
import concourse.bass as bass
from concourse import mybir
from contextlib import ExitStack


def macaron_kernel(nc, x_in, wq_in, wk_in, wv_in, wo_in, router_in, w1_in, w2_in, gate_up_in,
                   down_in, shared_gate_in, out):
    fp32 = mybir.dt.float32
    fp32r = mybir.dt.float32r
    int32 = mybir.dt.int32
    ALU = mybir.AluOpType
    ACT = mybir.ActivationFunctionType
    AX = mybir.AxisListType
    ds = bass.ds

    B, S, D = x_in.shape
    E, _, F = w1_in.shape
    HD = 64
    H = wq_in.shape[1] // HD
    BLK = 64
    P = 128
    QT = S // P
    NBLK = S // BLK
    PAIRS = H // 2
    UNITS = B * H
    NE = E + 1
    NH = NE + 1
    EPS = 1e-5
    RSQRT_SEED = float(0x5F3759DF)
    FAR = -3.0e38
    TINY = 2.0 ** -60
    TILES = B * QT
    CR = HD + 2 * NBLK

    ctx = ExitStack()
    with ctx:
        def sb(name, shape, dt=fp32):
            return ctx.enter_context(nc.sbuf_tensor(name, shape, dt))

        def sem(name):
            return ctx.enter_context(nc.semaphore(name))

        x = sb("x", [P, TILES * D])
        xT_hi = sb("xT_hi", [D, B * S], fp32r)
        xT_lo = sb("xT_lo", [D, B * S], fp32r)
        w1_hi = sb("w1_hi", [D, NH * F], fp32r)
        w1_lo = sb("w1_lo", [D, NH * F], fp32r)
        w2 = sb("w2", [F, NE * D])
        router_hi = sb("router_hi", [D, P], fp32r)
        router_lo = sb("router_lo", [D, P], fp32r)
        wqkv = sb("wqkv", [D, 3, H * HD])
        wo = sb("wo", [2 * HD, PAIRS * D])
        oT = sb("oT", [2 * HD, B * PAIRS * S])
        w_raw = oT[:, 0:NH * F]
        router_raw = oT[:, 2048:2048 + P]
        block_raw = oT[HD:CR, 8192:8192 + S]
        xs_hi = sb("xs_hi", [D, S], fp32r)
        xs_lo = sb("xs_lo", [D, S], fp32r)
        w_hi = sb("w_hi", [D, 2, P], fp32r)
        w_lo = sb("w_lo", [D, 2, P], fp32r)
        wv_hi = sb("wv_hi", [D, 2 * P], fp32r)
        wv_lo = sb("wv_lo", [D, 2 * P], fp32r)
        qk_pair = sb("qk_pair", [P, 4, S])
        NU = 4
        q_hh = [sb(f"q_hh{n}", [2 * HD, S], fp32r) for n in range(NU)]
        k_hl = [sb(f"k_hl{n}", [2 * HD, S], fp32r) for n in range(NU)]
        q_lc = [sb(f"q_lc{n}", [CR, S], fp32r) for n in range(NU)]
        k_hb = [sb(f"k_hb{n}", [CR, S], fp32r) for n in range(NU)]
        v_next = sb("v_next", [P, QT, 2 * P])
        v_st = [sb(f"v_st{n}", [P, QT, P]) for n in range(2)]
        e_sb = sb("e_sb", [P, 2, 2 * S])
        half = sb("half", [P, 2, 2 * NBLK, BLK // 2])
        pTs = [sb(f"pT{n}", [P, QT, S]) for n in range(2)]
        pT = pTs[0]
        hid = e_sb[:, :, :].rearrange("p g (n s) -> p (g n) s", n=2)
        xn = pTs[1]
        logitT = pT[0:NE, :, :].rearrange("e b s -> e (b s)")
        rt = qk_pair[:, :, :].rearrange("p a (b c) -> p (a b) c", c=TILES * 16)
        comb = rt[:, 6, :].rearrange("p (t e) -> p t e", e=16)
        ident = sb("ident", [P, P])
        stats = sb("stats", [P, TILES, 6])
        rs = sb("rs", [P, 4, TILES])
        reset0 = sb("reset0", [P, TILES * NBLK])
        reset1 = sb("reset1", [P, QT * NBLK])
        far0 = sb("far0", [P, QT * NBLK])
        bmax = sb("bmax", [P, 2, QT * NBLK])
        bsum = sb("bsum", [P, QT * NBLK])
        nm = sb("nm", [P, 2, QT])
        tiny = sb("tiny", [P, 1])
        st = sb("st", [P, 5, QT * NBLK])
        ctile = sb("ctile", [P, QT, CR])

        psA = ctx.enter_context(nc.psum_tensor("psA", [P, 4, S], fp32))
        psB = [ctx.enter_context(nc.psum_tensor(f"psB{n}", [P, S], fp32)) for n in range(2)]
        psY = ctx.enter_context(nc.psum_tensor("psY", [P, S], fp32))
        psM = ctx.enter_context(nc.psum_tensor("psM", [P, S], fp32))
        y_banks = (psY, psB[0], psB[1])

        x_in_s = [sem(f"x_in_s{b}") for b in range(B)]
        w_in_s = sem("w_in_s"); wa_in_s = sem("wa_in_s")
        r_zero_s = sem("r_zero_s"); r_in_s = sem("r_in_s")
        consts_s = sem("consts_s"); pool_step = sem("pool_step"); split_s = sem("split_s")
        router_s = sem("router_s")
        dve_step = sem("dve_step")
        stats_s = sem("stats_s"); xn_s = sem("xn_s")
        xT_ps = sem("xT_ps"); xT_hi_s = sem("xT_hi_s"); xT_lo_s = sem("xT_lo_s")
        logit_ps = sem("logit_ps"); logitT_s = sem("logitT_s"); lt_ps = sem("lt_ps")
        rexp_in = sem("rexp_in"); rexp_s = sem("rexp_s")
        ident_s = sem("ident_s")
        hid_ps = sem("hid_ps"); silu_s = sem("silu_s"); up_s = sem("up_s")
        y_ps = sem("y_ps"); x_s = sem("x_s")
        xs_s = sem("xs_s"); wqk_s = sem("wqk_s"); wv_s = sem("wv_s")
        q_ps = sem("q_ps"); q_hi_s = sem("q_hi_s"); q_lo_s = sem("q_lo_s")
        k_ps = sem("k_ps"); k_hi_s = sem("k_hi_s"); k_lo_s = sem("k_lo_s")
        v_ps = sem("v_ps"); v_s = sem("v_s"); v_moved = [sem(f"v_moved{n}") for n in range(2)]
        qk0_s = sem("qk0_s"); qk1_s = sem("qk1_s")
        s_ps = sem("s_ps"); nm_s = sem("nm_s"); e_s = sem("e_s"); half_s = sem("half_s")
        bsum_s = sem("bsum_s"); ln_in = sem("ln_in"); ln_s = sem("ln_s")
        c_s = sem("c_s"); cT_ps = sem("cT_ps"); cT_s = sem("cT_s")
        sT_ps = sem("sT_ps"); pT_s = sem("pT_s"); o_ps = sem("o_ps"); o_s = sem("o_s")
        zT_ps = sem("zT_ps"); zT_s = sem("zT_s"); z_ps = sem("z_ps"); z_s = sem("z_s")
        out_s = sem("out_s")

        block = ctx.enter_context(nc.Block())

        QK_DMAS = 6
        FFN_LAG = 1
        HEAD_START = 4

        def raw(ap):
            return ap.bitcast(fp32)

        def past(eng, semaphore, count):
            if not isinstance(count, int) or count > 0:
                eng.wait_ge(semaphore, count)

        TURNS = UNITS // NU

        def in_slots(eng, slot, after={}):
            for i in (-1, 0):
                for s in range(NU):
                    slot(i, s)
                    if i < 0 and s in after:
                        after[s]()
            with eng.Fori(1, TURNS - 1) as i:
                for s in range(NU):
                    slot(i, s)
            for s in range(NU):
                slot(TURNS - 1, s)

        def unit(i, k):
            return i * NU + k

        def pair(i, k):
            return i * (NU // 2) + k // 2

        def is_unit(u):
            return not isinstance(u, int) or 0 <= u < UNITS

        def is_turn(i):
            return not isinstance(i, int) or 0 <= i < TURNS

        def is_pair(p):
            return not isinstance(p, int) or 0 <= p < UNITS // 2

        @block.sync
        def _(sp):
            xv = x[:, :].rearrange("p (t d) -> p t d", d=D)
            for b in range(B):
                sp.dma_start(xv[:, b * QT:(b + 1) * QT, :],
                             x_in[b].rearrange("(t p) d -> p t d", p=P)).then_inc(x_in_s[b], 16)
            for n, w in enumerate((wq_in, wk_in, wv_in)):
                sp.dma_start(wqkv[:, n, :], w).then_inc(wa_in_s, 16)
            sp.dma_start(wo[:, :].rearrange("r (h d) -> r h d", d=D),
                         wo_in.rearrange("(h r) d -> r h d", r=2 * HD)).then_inc(wa_in_s, 16)

            def q_copies(n, h, done):
                rows = slice(h * HD, (h + 1) * HD)
                for to in range(2):
                    sp.dma_start(raw(q_hh[n][to * HD:(to + 1) * HD, :]), qk_pair[rows, 0, :])\
                      .then_inc(done, 16)
                sp.dma_start(raw(q_lc[n][0:HD, :]), qk_pair[rows, 1, :]).then_inc(done, 16)

            def k_copies(n, h, done):
                rows = slice(h * HD, (h + 1) * HD)
                sp.dma_start(raw(k_hl[n][0:HD, :]), qk_pair[rows, 2, :]).then_inc(done, 16)
                sp.dma_start(raw(k_hb[n][0:HD, :]), qk_pair[rows, 2, :]).then_inc(done, 16)
                sp.dma_start(raw(k_hl[n][HD:2 * HD, :]), qk_pair[rows, 3, :]).then_inc(done, 16)

            def load_xs(b):
                sp.wait_ge(xT_hi_s, B + 1 + b)
                sp.wait_ge(xT_lo_s, B + 1 + b)
                sp.dma_start(raw(xs_hi[:, :]), raw(xT_hi[:, ds(b * S, S)])).then_inc(xs_s, 16)
                sp.dma_start(raw(xs_lo[:, :]), raw(xT_lo[:, ds(b * S, S)])).then_inc(xs_s, 16)

            def v_copy(which):
                sp.dma_start(v_st[which][:, :, :], v_next[:, :, which * P:(which + 1) * P])\
                  .then_inc(v_moved[which], 16)

            def slot(i, s):
                u, p = unit(i, s), pair(i, s + NU)
                if s == 0 and is_turn(i):
                    past(sp, o_ps, pair(i, s))
                    v_copy(1)
                if s == 0 and is_turn(i) and is_turn(i + 1):
                    load_xs((i + 1) // (H // NU))
                if s == 3 and is_turn(i + 1):
                    sp.wait_ge(v_s, 2 * i + 4)
                    v_copy(0)
                if is_pair(p):
                    done = (qk0_s, qk1_s)[s % 2]
                    if s % 2 == 0 and isinstance(i, int) and i < 0:
                        sp.wait_ge(q_lo_s, p + 1)
                    elif s % 2 == 0:
                        sp.wait_ge(k_lo_s, p + 1)
                    else:
                        past(sp, sT_ps, QT * (u + 1))
                    q_copies(s, s % 2, done)
                    if s % 2 == 0 and isinstance(i, int) and i < 0:
                        sp.wait_ge(k_lo_s, p + 1)
                    k_copies(s, s % 2, done)

            in_slots(sp, slot)
            for b in range(B):
                sp.wait_ge(x_s, NE * (B + b + 1))
                sp.dma_start(out[b].rearrange("(t p) d -> p t d", p=P),
                             xv[:, b * QT:(b + 1) * QT, :]).then_inc(out_s, 16)
            sp.wait_ge(out_s, 16 * B)

        @block.gpsimd
        def _(pool):
            steps = [0]

            def step(ins):
                steps[0] += 1
                ins.then_inc(pool_step, 1)
                pool.wait_ge(pool_step, steps[0])

            pool.memset(router_raw, 0.0).then_inc(r_zero_s, 1)
            pool.wait_ge(r_zero_s, 1)
            step(pool.memset(ident[:, :], 0.0))
            pool.affine_select(out=ident[:, :], in_=ident[:, :], compare_op=ALU.not_equal, fill=1.0,
                               base=0, pattern=[[-1, P]], channel_multiplier=1).then_inc(ident_s, 1)
            pool.wait_ge(ident_s, 1)
            for tile, value in ((tiny[:, :], TINY), (reset0[:, :], 1.0), (reset1[:, :], 1.0),
                                (far0[:, :], 0.0), (ctile[:, :, :], 0.0), (block_raw, 0.0)):
                step(pool.memset(tile, value))
            blv = block_raw.rearrange("r (j k) -> r j k", k=BLK)
            for twin in range(2):
                step(pool.affine_select(out=blv, in_=blv, compare_op=ALU.not_equal, fill=1.0,
                                        base=twin * NBLK, pattern=[[1, NBLK], [0, BLK]],
                                        channel_multiplier=-1))
            for tile, at, value in ((reset0, 0, 0.0), (reset1, NBLK - 1, 0.0), (far0, 0, FAR)):
                tv = tile[:, :].rearrange("p (t j) -> p t j", j=NBLK)
                step(pool.memset(tv[:, :, at:at + 1], value))
            for n in range(NU):
                pool.tensor_copy(k_hb[n][HD:CR, :], block_raw).then_inc(consts_s, 1)
                pool.wait_ge(consts_s, n + 1)

            def qk_split(p):
                past(pool, k_ps, p)
                src = wqkv[:, 0:2, ds((p % PAIRS) * P, P)]
                return src, w_hi[:, :, :], w_lo[:, :, :], wqk_s, 2 * p + 1

            def v_split(i):
                past(pool, v_ps, 2 * i)
                src = wqkv[:, 2, ds((i % (H // NU)) * (2 * P), 2 * P)]
                return src, wv_hi[:, :], wv_lo[:, :], wv_s, 2 * i + 1

            def split_hi(src, hi, lo, done, count):
                pool.tensor_copy(hi, src).then_inc(done, 1)
                pool.wait_ge(done, count)

            def split_lo(src, hi, lo, done, count):
                pool.tensor_tensor(lo, src, raw(hi), ALU.subtract).then_inc(done, 1)

            def slot(i, s):
                n = unit(i, s + 2)
                job = None
                if s % 2 == 1 and is_pair(pair(i, s + 5)):
                    job = qk_split(pair(i, s + 5))
                if s == 0 and is_turn(i + 1):
                    job = v_split(i + 1)
                if job:
                    split_hi(*job)
                for g in range(2):
                    if is_unit(n):
                        pool.wait_ge(e_s, 2 * n + g + 1)
                        past(pool, bsum_s, 2 * n + g - 1)
                        ev = e_sb[:, g, :].rearrange("p (j k) -> p j k", k=BLK)
                        pool.tensor_tensor(half[:, g, :, :], ev[:, :, 0:BLK // 2],
                                           ev[:, :, BLK // 2:BLK], ALU.add).then_inc(half_s, 1)
                    if g == 0 and job:
                        split_lo(*job)

            pool.wait_ge(split_s, 1)
            pool.tensor_tensor(router_lo[:, :], router_raw, raw(router_hi[:, :]), ALU.subtract)\
                .then_inc(router_s, 1)
            pool.wait_ge(split_s, 2)
            pool.tensor_tensor(w1_lo[:, :], w_raw, raw(w1_hi[:, :]), ALU.subtract).then_inc(split_s, 1)
            pool.wait_ge(wa_in_s, 16 * 4)
            job = qk_split(0)
            split_hi(*job)
            split_lo(*job)
            in_slots(pool, slot)

        @block.scalar
        def _(act):
            act.wait_ge(r_zero_s, 1)
            act.dma_start(router_raw[:, 0:E], router_in).then_inc(r_in_s, 16)
            act.dma_start(router_raw[:, E:NE], shared_gate_in).then_inc(r_in_s, 16)
            act.dma_start(w_raw[:, 0:E * F].rearrange("d (e f) -> d e f", f=F),
                          w1_in.rearrange("e d f -> d e f")).then_inc(w_in_s, 16)
            act.dma_start(w_raw[:, E * F:NH * F], gate_up_in).then_inc(w_in_s, 16)
            act.dma_start(w2[:, 0:E * D].rearrange("f (e d) -> f e d", d=D),
                          w2_in.rearrange("e f d -> f e d")).then_inc(w_in_s, 16)
            act.dma_start(w2[:, E * D:NE * D], down_in).then_inc(w_in_s, 16)

            def turned(norm, batches):
                for b in batches:
                    act.wait_ge(xT_ps, B * norm + b + 1)
                    nc.scalar.activation(xT_hi[:, b * S:(b + 1) * S], psA[:, b, :], ACT.Copy)\
                        .then_inc(xT_hi_s, 1)

            def ffn(phase):
                if phase == 0:
                    turned(0, range(B))
                for b in range(B):
                    if phase == 1 and b in (0, B - 1):
                        turned(2, range(B - 2 + b // (B - 1), B - 1 + b // (B - 1)))
                    act.wait_ge(logit_ps, B * phase + b + 1)
                    nc.scalar.activation(logitT[:, b * S:(b + 1) * S], (psM, psY)[b % 2][0:NE, :], ACT.Copy)\
                        .then_inc(logitT_s, 1)
                act.wait_ge(rexp_in, phase + 1)
                lv = rt[:, 1, :].rearrange("p (t e) -> p t e", e=16)
                nc.scalar.activation(lv[:, :, 0:NE], lv[:, :, 0:NE], ACT.Exp).then_inc(rexp_s, 1)

                def experts(b):
                    g = b + B * phase
                    for e in range(NE):
                        act.wait_ge(hid_ps, NH * g + e + 1)
                        past(act, y_ps, NE * g + e - 2)
                        nc.scalar.activation(hid[:, e % 3, :], psA[:, e % 4, :], ACT.Silu)\
                            .then_inc(silu_s, 1)

                experts(0)
                with act.Fori(1, B) as b:
                    experts(b)

            act.wait_ge(w_in_s, 16 * 4)
            act.wait_ge(r_in_s, 32)
            nc.scalar.activation(router_hi[:, :], router_raw, ACT.Copy).then_inc(split_s, 1)
            nc.scalar.activation(w1_hi[:, :], w_raw, ACT.Copy).then_inc(split_s, 1)
            ffn(0)
            act.preload_act_table_set("natural_log_exp_and_others")
            turned(1, range(1))

            def output(p):
                act.wait_ge(o_ps, p + 1)
                nc.scalar.activation(oT[:, ds(p * S, S)], psY[:, :], ACT.Copy).then_inc(o_s, 1)

            def slot(i, s):
                u, m, n = unit(i, s), unit(i, s + 1), unit(i, s + 2)

                def exps(g):
                    if is_unit(n):
                        act.wait_ge(nm_s, 2 * n + g + 1)
                        past(act, half_s, 2 * n + g - 1)
                        for q in (2 * g, 2 * g + 1):
                            ins = nc.scalar.activation(e_sb[:, g, (q % 2) * S:(q % 2 + 1) * S],
                                                       psA[:, q, :], ACT.Exp,
                                                       bias=nm[:, s % 2, q:q + 1])
                        ins.then_inc(e_s, 1)

                def weighted(k):
                    if is_unit(u):
                        act.wait_ge(sT_ps, QT * u + k + 1)
                        nc.scalar.activation(pTs[s % 2][:, k, :], psB[k % 2][:, :], ACT.Exp)\
                            .then_inc(pT_s, 1)

                def last_output():
                    if s % 2 == 0 and is_pair(pair(i, s - 2)):
                        output(pair(i, s - 2))

                p = pair(i, s + 4)
                qk = s % 2 == 0 and is_pair(p)

                def q_or_v():
                    if qk:
                        act.wait_ge(q_ps, p + 1)
                        past(act, qk0_s, 16 * QK_DMAS * p)
                        past(act, qk1_s, 16 * QK_DMAS * p)
                        nc.scalar.activation(qk_pair[:, 0, :].bitcast(fp32r), psM[:, :], ACT.Copy,
                                             scale=HD ** -0.5).then_inc(q_hi_s, 1)
                    if s % 2 == 1 and is_turn(i + 1):
                        r = s // 2
                        act.wait_ge(v_ps, 2 * i + 3 + r)
                        for moved in v_moved:
                            past(act, moved, 16 * (i + 1))
                        nc.scalar.activation(v_next[:, 2 * r:2 * r + 2, :]
                                             .rearrange("p t d -> p (t d)"),
                                             psM[:, :], ACT.Copy).then_inc(v_s, 1)

                def k_hi():
                    if qk:
                        act.wait_ge(k_ps, p + 1)
                        nc.scalar.activation(qk_pair[:, 2, :].bitcast(fp32r), psM[:, :], ACT.Copy)\
                            .then_inc(k_hi_s, 1)

                def logs():
                    if is_unit(m):
                        act.wait_ge(ln_in, m + 1)
                        nc.scalar.activation(st[:, 2, :], st[:, 2, :], ACT.Ln, bias=tiny[:, 0:1])\
                            .then_inc(ln_s, 1)

                def c_rows():
                    if is_unit(m):
                        act.wait_ge(cT_ps, m + 1)
                        nc.scalar.activation(q_lc[(s + 1) % NU][HD:CR, :], psA[HD:CR, 0, :],
                                             ACT.Copy).then_inc(cT_s, 1)

                if s % 2 == 0:
                    weighted(0)
                    weighted(1)
                    last_output()
                    logs()
                    q_or_v()
                    exps(0)
                    weighted(2)
                    weighted(3)
                    c_rows()
                    k_hi()
                    exps(1)
                else:
                    weighted(0)
                    weighted(1)
                    q_or_v()
                    logs()
                    exps(0)
                    weighted(2)
                    weighted(3)
                    c_rows()
                    exps(1)

            act.wait_ge(consts_s, NU)
            in_slots(act, slot, {0: lambda: turned(1, range(1, B))})
            output(UNITS // 2 - 1)

            for b in range(B):
                if b >= 2:
                    turned(2, range(b - 2, b - 1))
                act.wait_ge(zT_ps, b + 1)
                nc.scalar.activation(pT[:, b, :], psA[:, b, :], ACT.Copy).then_inc(zT_s, 1)
            ffn(1)

        @block.vector
        def _(dve):
            V = nc.vector
            base, at, turn = [0], [0], [None, 0]

            def post(ins):
                at[0] += 1
                ins.then_inc(dve_step, 1)
                return at[0]

            def need(mark):
                dve.wait_ge(dve_step, base[0] + mark if turn[0] is None
                            else turn[0] * turn[1] + (base[0] + mark))

            def step(ins):
                need(post(ins))

            def stats_of(norm, b, semaphore, count):
                dve.wait_ge(semaphore, count)
                for t in range(QT):
                    ins = V.bn_stats(stats[:, b * QT + t, :] if isinstance(b, int)
                                     else stats[:, ds(b * QT + t, 1), :].rearrange("p a c -> p (a c)"),
                                     x[:, ds(b * (QT * D) + t * D, D)])
                ins.then_inc(stats_s, 1)

            def scales(norm, first, end):
                dve.wait_ge(stats_s, B * norm + end)
                ts = slice(first * QT, end * QT)
                mean, var, y, a = (rs[:, k, ts] for k in range(4))
                me, qe, mo, qo = (stats[:, ts, k] for k in (1, 2, 4, 5))
                V.tensor_tensor(a, me, mo, ALU.subtract)
                V.tensor_tensor(mean, me, mo, ALU.add)
                step(V.tensor_tensor(var, qe, qo, ALU.add))
                V.scalar_tensor_tensor(a, a, 0.25, a, ALU.mult, ALU.mult)
                V.tensor_scalar(mean, mean, 0.5, None, ALU.mult)
                step(V.tensor_scalar(var, var, 1.0 / D, EPS, ALU.mult, ALU.add))
                step(V.tensor_tensor(var, var, a, ALU.add))
                step(V.tensor_scalar(y.bitcast(int32), var.bitcast(int32), -0.5, RSQRT_SEED,
                                     ALU.mult, ALU.add))
                for _ in range(3):
                    step(V.scalar_tensor_tensor(a, y, -0.5, var, ALU.mult, ALU.mult))
                    step(V.tensor_tensor(a, a, y, ALU.mult))
                    step(V.scalar_tensor_tensor(y, a, 1.5, y, ALU.add, ALU.mult))

            def lo(norm, b):
                dve.wait_ge(xT_hi_s, B * norm + b + 1)
                V.tensor_tensor(xT_lo[:, b * S:(b + 1) * S], psA[:, b, :],
                                raw(xT_hi[:, b * S:(b + 1) * S]), ALU.subtract).then_inc(xT_lo_s, 1)

            def normed(norm, b):
                past(dve, xT_ps, B * (norm - 1) + b + 1)
                mean, y = rs[:, 0, :], rs[:, 2, :]
                for t in range(QT):
                    k = QT * b + t
                    ins = V.tensor_scalar(xn[:, b, t * D:(t + 1) * D], x[:, k * D:(k + 1) * D],
                                          mean[:, k:k + 1], y[:, k:k + 1], ALU.subtract, ALU.mult)
                ins.then_inc(xn_s, 1)

            def all_normed(norm):
                for b in range(B):
                    normed(norm, b)
                    if b == B - 2:
                        lo(norm, 0)

            def other_los(norm):
                for b in range(1, B):
                    lo(norm, b)

            def router(phase):
                logit, ls, m, sel1, sel2 = (rt[:, n, :].rearrange("p (t e) -> p t e", e=16)
                                            for n in range(5))
                w = comb
                flat = rt[:, 7, :]
                mask_f, count_f = flat[:, 0:TILES * E], flat[:, TILES * E:2 * TILES * E]
                mask = mask_f.rearrange("p (t e) -> p t e", e=E)
                count = count_f.rearrange("p (t e) -> p t e", e=E)

                def over_e(v):
                    return v.broadcast_to([P, TILES, E])

                dve.wait_ge(lt_ps, phase + 1)
                step(V.tensor_copy(logit[:, :, 0:NE],
                                   psM[:, 0:TILES * 16].rearrange("p (t e) -> p t e", e=16)[:, :, 0:NE]))
                step(V.tensor_reduce(m[:, :, 8:9], logit[:, :, 0:E], AX.X, ALU.max))
                V.tensor_scalar(ls[:, :, E:NE], logit[:, :, E:NE], -1.0, None, ALU.mult)
                V.tensor_tensor(ls[:, :, 0:E], logit[:, :, 0:E], over_e(m[:, :, 8:9]), ALU.subtract)\
                 .then_inc(rexp_in, 1)
                step(V.tensor_tensor(w[:, :, 0:E], logit[:, :, 0:E], over_e(m[:, :, 8:9]), ALU.subtract))

                def first_of(dst):
                    step(V.tensor_tensor_scan(count_f, reset0[:, 0:TILES * E], mask_f, 0.0,
                                              ALU.mult, ALU.add))
                    step(V.scalar_tensor_tensor(dst[:, :, 0:E], count, 1.0, mask,
                                                ALU.is_equal, ALU.mult))

                step(V.tensor_scalar(mask, w[:, :, 0:E], 0.0, None, ALU.is_equal))
                first_of(sel1)
                step(V.scalar_tensor_tensor(w[:, :, 0:E], sel1[:, :, 0:E], FAR, w[:, :, 0:E],
                                            ALU.mult, ALU.add))
                step(V.tensor_reduce(m[:, :, 8:9], w[:, :, 0:E], AX.X, ALU.max))
                step(V.tensor_tensor(mask, w[:, :, 0:E], over_e(m[:, :, 8:9]), ALU.is_equal))
                first_of(sel2)
                step(V.tensor_tensor(sel1[:, :, 0:E], sel1[:, :, 0:E], sel2[:, :, 0:E], ALU.add))
                dve.wait_ge(rexp_s, phase + 1)
                V.tensor_scalar(m[:, :, 10:11], ls[:, :, E:NE], 1.0, None, ALU.add)
                step(V.tensor_reduce(m[:, :, 9:10], ls[:, :, 0:E], AX.X, ALU.add))
                step(V.reciprocal(m[:, :, 11:13], m[:, :, 9:11]))
                step(V.scalar_tensor_tensor(w[:, :, 0:E], ls[:, :, 0:E], 0.5, sel1[:, :, 0:E],
                                            ALU.mult, ALU.mult))
                V.tensor_tensor(w[:, :, 0:E], w[:, :, 0:E], over_e(m[:, :, 11:12]), ALU.mult)
                step(V.tensor_scalar(w[:, :, E:NE], m[:, :, 12:13], 0.5, None, ALU.mult))

            def ffn(phase):
                def gate(b):
                    g = b + B * phase
                    dve.wait_ge(silu_s, NE * (g + 1))
                    dve.wait_ge(hid_ps, NH * (g + 1))
                    past(dve, y_ps, NE * g)
                    V.tensor_tensor(hid[:, 3, :], hid[:, (NE - 1) % 3, :], psA[:, (NH - 1) % 4, :],
                                    ALU.mult).then_inc(up_s, 1)

                def add(b, e):
                    g = b + B * phase
                    dve.wait_ge(y_ps, NE * g + e + 1)
                    past(dve, x_s, NE * g + e)
                    for t in range(QT):
                        xt = x[:, ds(b * (QT * D) + t * D, D)]
                        weight = comb[:, ds(b * QT + t, 1), e:e + 1].rearrange("p a e -> p (a e)")
                        ins = V.scalar_tensor_tensor(xt, y_banks[e % 3][:, t * D:(t + 1) * D],
                                                     weight, xt, ALU.mult, ALU.add)
                    ins.then_inc(x_s, 1)

                def experts(b, first):
                    for e in range(NE):
                        if e == NE - FFN_LAG - 1:
                            gate(b)
                        add(b, e)
                        if e == 2 and phase == 0 and not first:
                            stats_of(1, b - 1, x_s, NE * b)

                if phase == 0:
                    all_normed(0)
                    other_los(0)
                    step(V.memset(rt[:, :, :], 0.0))
                    dve.wait_ge(consts_s, NU)
                router(phase)
                experts(0, True)
                with dve.Fori(1, B) as b:
                    experts(b, False)

            for b in range(B):
                stats_of(0, b, x_in_s[b], 16)
            scales(0, 0, B)
            ffn(0)
            stats_of(1, B - 1, x_s, NE * B)
            scales(1, 0, B)
            all_normed(1)

            def tiles(ap):
                return ap.rearrange("p (t j) -> p t j", j=NBLK)

            def each(ap):
                return ap.rearrange("p (t o) -> p t o", o=1).broadcast_to([P, QT, NBLK])

            def slot(i, s):
                m, n = unit(i, s + 1), unit(i, s + 2)
                p = pair(i, s + 4)
                qk = s % 2 == 0 and is_pair(p)
                pm, dd, lsum, back, c = (st[:, k, :] for k in range(5))
                bmax_m, nm_m = bmax[:, (s + 1) % 2, :], nm[:, (s + 1) % 2, :]
                bmax_n, nm_n = bmax[:, s % 2, :], nm[:, s % 2, :]

                def sums(g):
                    dve.wait_ge(half_s, 2 * m + g + 1)
                    V.tensor_reduce(bsum[:, g * 2 * NBLK:(g + 1) * 2 * NBLK], half[:, g, :, :],
                                    AX.X, ALU.add).then_inc(bsum_s, 1)

                def maxima(g):
                    dve.wait_ge(s_ps, 2 * n + g + 1)
                    return post(V.tensor_reduce(
                        bmax_n[:, g * 2 * NBLK:(g + 1) * 2 * NBLK],
                        psA[:, 2 * g:2 * g + 2, :].rearrange("p t (j k) -> p (t j) k", k=BLK),
                        AX.X, ALU.max))

                def negated(g, mark):
                    need(mark)
                    V.tensor_reduce(nm_n[:, 2 * g:2 * g + 2], tiles(bmax_n)[:, 2 * g:2 * g + 2, :],
                                    AX.X, ALU.max, negate=True).then_inc(nm_s, 1)

                marks = {}

                def sums_up_to(g):
                    if not is_unit(m):
                        return
                    sums(g)
                    if g == 0:
                        marks["pm"] = post(V.tensor_tensor_scan(pm, far0[:, :], bmax_m, FAR,
                                                                ALU.add, ALU.max))
                    else:
                        need(marks["pm"])
                        marks["dd"] = post(V.tensor_tensor(tiles(dd), tiles(pm), each(nm_m), ALU.add))
                        dve.wait_ge(bsum_s, 2 * m + 2)
                        V.tensor_tensor_scan(lsum, reset0[:, 0:QT * NBLK], bsum[:, :], 0.0,
                                             ALU.mult, ALU.add).then_inc(ln_in, 1)

                def weights():
                    if not is_unit(m):
                        return
                    dve.wait_ge(ln_s, m + 1)
                    need(marks["dd"])
                    step(V.tensor_tensor(lsum, lsum, dd, ALU.subtract))
                    step(V.tensor_tensor_scan(back[:, ::-1], reset1[:, ::-1], lsum[:, ::-1], 0.0,
                                              ALU.mult, ALU.add))
                    V.tensor_tensor(ctile[:, :, HD:HD + NBLK].bitcast(fp32r), each(nm_m), tiles(back),
                                    ALU.subtract)
                    step(V.tensor_tensor(tiles(c), each(nm_m), tiles(back), ALU.subtract))
                    V.tensor_tensor(ctile[:, :, HD + NBLK:CR], tiles(c), ctile[:, :, HD:HD + NBLK],
                                    ALU.subtract).then_inc(c_s, 1)

                def row_maxima(g):
                    if is_unit(n):
                        negated(g, maxima(g))

                def q_lo():
                    if qk:
                        dve.wait_ge(q_hi_s, p + 1)
                        V.scalar_tensor_tensor(qk_pair[:, 1, :].bitcast(fp32r), psM[:, :], HD ** -0.5,
                                               qk_pair[:, 0, :], ALU.mult, ALU.subtract)\
                         .then_inc(q_lo_s, 1)

                def k_lo():
                    if qk:
                        dve.wait_ge(k_hi_s, p + 1)
                        V.tensor_tensor(qk_pair[:, 3, :].bitcast(fp32r), psM[:, :], qk_pair[:, 2, :],
                                        ALU.subtract).then_inc(k_lo_s, 1)

                if s % 2 == 0:
                    sums_up_to(0)
                    sums_up_to(1)
                    row_maxima(0)
                    weights()
                    q_lo()
                    row_maxima(1)
                    k_lo()
                else:
                    sums_up_to(0)
                    row_maxima(0)
                    sums_up_to(1)
                    weights()
                    row_maxima(1)

            SLOT_MARKS = 7
            for i in (-1, 0):
                for s in range(NU):
                    slot(i, s)
                    if (i, s) == (-1, 0):
                        other_los(1)
            base[0] += at[0] - NU * SLOT_MARKS
            at[0] = 0
            with dve.Fori(1, TURNS - 1) as i:
                turn[:] = [i, NU * SLOT_MARKS]
                for s in range(NU):
                    slot(i, s)
            assert at[0] == NU * SLOT_MARKS, at[0]
            turn[0] = None
            base[0] += NU * SLOT_MARKS * (TURNS - 1)
            at[0] = 0
            for s in range(NU):
                slot(TURNS - 1, s)

            for b in range(B):
                dve.wait_ge(z_ps, b + 1)
                xb = x[:, b * (QT * D):(b + 1) * (QT * D)]
                V.tensor_tensor(xb, xb, psB[b % 2][:, :], ALU.add).then_inc(z_s, 1)
                stats_of(2, b, z_s, b + 1)
                if b >= 1:
                    lo(2, b - 1)
                scales(2, b, b + 1)
                normed(2, b)
            lo(2, B - 1)
            ffn(1)

        @block.tensor
        def _(pe):
            T = nc.tensor

            def three(o, w_hi_, w_lo_, r_hi, r_lo):
                T.matmul(o, w_hi_, r_hi, start=True, stop=False)
                T.matmul(o, w_hi_, r_lo, start=False, stop=False)
                return T.matmul(o, w_lo_, r_hi, start=False, stop=True)

            def turn_x(norm, batches):
                for b in batches:
                    pe.wait_ge(xn_s, B * norm + b + 1)
                    for t in range(QT):
                        ins = T.transpose(psA[:, b, t * P:(t + 1) * P], xn[:, b, t * D:(t + 1) * D],
                                          ident[:, :])
                    ins.then_inc(xT_ps, 1)

            def ffn(phase):
                def hidden(b, j):
                    g = b + B * phase
                    if j >= 4:
                        pe.wait_ge(silu_s, NE * g + j - 3)
                    elif j == 1:
                        past(pe, up_s, g)
                    else:
                        past(pe, silu_s, NE * g)
                    three(psA[:, j % 4, :], w1_hi[:, j * F:(j + 1) * F], w1_lo[:, j * F:(j + 1) * F],
                          xT_hi[:, ds(b * S, S)], xT_lo[:, ds(b * S, S)]).then_inc(hid_ps, 1)

                def second(b, e):
                    g = b + B * phase
                    if e < NE - 1:
                        pe.wait_ge(silu_s, NE * g + e + 1)
                        src = hid[:, e % 3, :]
                    else:
                        pe.wait_ge(up_s, g + 1)
                        src = hid[:, 3, :]
                    past(pe, x_s, NE * g + e - 2)
                    for t in range(QT):
                        ins = T.matmul(y_banks[e % 3][:, t * D:(t + 1) * D], src[:, t * P:(t + 1) * P],
                                       w2[:, e * D:(e + 1) * D], start=True, stop=True)
                    ins.then_inc(y_ps, 1)

                def experts(b, first):
                    for e in range(NE):
                        if not (first and e < HEAD_START):
                            hidden(b, e)
                        if e == NE - 1:
                            hidden(b, NE)
                        if e >= FFN_LAG:
                            second(b, e - FFN_LAG)
                        elif not first:
                            second(b - 1, NE + e - FFN_LAG)

                if phase == 0:
                    turn_x(0, range(B))
                    pe.wait_ge(router_s, 1)
                for b in range(B):
                    if phase == 1 and b == B - 1:
                        for j in range(B - 1):
                            hidden(0, j)
                        turn_x(2, range(B - 1, B))
                    pe.wait_ge(xT_lo_s, 2 * B * phase + b + 1)
                    if b >= 2:
                        pe.wait_ge(logitT_s, B * phase + b - 1)
                    three((psM, psY)[b % 2][:, :], router_hi[:, :], router_lo[:, :],
                          xT_hi[:, b * S:(b + 1) * S], xT_lo[:, b * S:(b + 1) * S]).then_inc(logit_ps, 1)
                if phase == 0:
                    pe.wait_ge(split_s, 3)
                    pe.wait_ge(w_in_s, 16 * 4)
                for j in range(phase * (B - 1), HEAD_START):
                    hidden(0, j)
                pe.wait_ge(logitT_s, B * (phase + 1))
                for t in range(TILES):
                    ins = T.transpose(psM[:, t * 16:t * 16 + NE], logitT[:, t * P:(t + 1) * P],
                                      ident[0:NE, 0:NE])
                ins.then_inc(lt_ps, 1)
                experts(0, True)
                with pe.Fori(1, B) as b:
                    experts(b, False)
                for e in range(NE - FFN_LAG, NE):
                    second(B - 1, e)

            pe.wait_ge(ident_s, 1)
            ffn(0)
            turn_x(1, range(1))
            pe.wait_ge(consts_s, NU)

            def product(which, k):
                for h in range(2):
                    rows = slice(h * HD, (h + 1) * HD)
                    ins = T.matmul(psY[rows, :], v_st[which][:, k, rows], pTs[h][:, k, :],
                                   start=(k == 0), stop=(k == QT - 1))
                if k == QT - 1:
                    ins.then_inc(o_ps, 1)

            def slot(i, s):
                u, m, n = unit(i, s), unit(i, s + 1), unit(i, s + 2)
                tn, tu = (s + 2) % NU, s % NU

                def scores(g):
                    if not is_unit(n):
                        return
                    if g == 0:
                        pe.wait_ge((qk0_s, qk1_s)[s % 2], 16 * QK_DMAS * (pair(i, s + 2) + 1))
                    past(pe, e_s, 2 * n + g - 1)
                    if g == 0:
                        past(pe, cT_s, u + 1)
                    for q in (2 * g, 2 * g + 1):
                        T.matmul(psA[:, q, :], q_hh[tn][:, q * P:(q + 1) * P], k_hl[tn][:, :],
                                 start=True, stop=False)
                    for q in (2 * g, 2 * g + 1):
                        ins = T.matmul(psA[:, q, :], q_lc[tn][0:HD, q * P:(q + 1) * P],
                                       k_hl[tn][0:HD, :], start=False, stop=True)
                    ins.then_inc(s_ps, 1)

                def scoresT(ks):
                    if is_unit(u):
                        for k in ks:
                            past(pe, pT_s, QT * u + k - 1)
                            T.matmul(psB[k % 2][:, :], k_hl[tu][:, k * P:(k + 1) * P],
                                     q_hh[tu][:, :], start=True, stop=False)

                def add_c(ks):
                    if is_unit(u):
                        if ks[0] == 0:
                            pe.wait_ge(cT_s, u + 1)
                        for k in ks:
                            T.matmul(psB[k % 2][:, :], k_hb[tu][:, k * P:(k + 1) * P],
                                     q_lc[tu][:, :], start=False, stop=True).then_inc(sT_ps, 1)

                def pv(k):
                    if s % 2 == 1 and k < QT // 2 and is_pair(pair(i, s)):
                        if k == 0:
                            pe.wait_ge(v_moved[s // 2], 16 * (i + 1))
                            past(pe, o_s, pair(i, s))
                        pe.wait_ge(pT_s, QT * u + k + 1)
                        product(s // 2, k)
                    if s % 2 == 0 and k >= QT // 2 and is_pair(pair(i, s - 2)):
                        pe.wait_ge(pT_s, QT * (u - 1) + k + 1)
                        product((s // 2 + 1) % 2, k)

                p = pair(i, s + 4)
                qk = s % 2 == 0 and is_pair(p)

                def project(which, done):
                    at = ds((p // PAIRS) * S, S)
                    three(psM[:, :], w_hi[:, which, :], w_lo[:, which, :], xT_hi[:, at], xT_lo[:, at])\
                        .then_inc(done, 1)

                def project_q_or_v():
                    if qk:
                        pe.wait_ge(wqk_s, 2 * p + 2)
                        past(pe, v_s, 2 * i + 2 + s // 2)
                        project(0, q_ps)
                    if s % 2 == 1 and is_turn(i + 1):
                        r = s // 2
                        pe.wait_ge(wv_s, 2 * (i + 2))
                        x_hi, x_lo = xT_hi, xT_lo
                        if not (isinstance(i, int) and i < 0):
                            pe.wait_ge(xs_s, 32 * (i + 1))
                            x_hi, x_lo = xs_hi, xs_lo
                        if is_pair(pair(i, s + 3)):
                            pe.wait_ge(k_lo_s, pair(i, s + 3) + 1)
                        for t in range(2):
                            tt = slice((2 * r + t) * P, (2 * r + t + 1) * P)
                            ins = three(psM[:, t * 2 * P:(t + 1) * 2 * P], x_hi[:, tt], x_lo[:, tt],
                                        wv_hi[:, :], wv_lo[:, :])
                        ins.then_inc(v_ps, 1)

                def project_k():
                    if qk:
                        pe.wait_ge(q_hi_s, p + 1)
                        pe.wait_ge(q_lo_s, p + 1)
                        project(1, k_ps)

                def turn_c():
                    if not is_unit(m):
                        return
                    pe.wait_ge(c_s, m + 1)
                    if is_unit(n):
                        pe.wait_ge(e_s, 2 * n + 1)
                    for q in range(QT):
                        ins = T.transpose(psA[0:CR, 0, q * P:(q + 1) * P], ctile[:, q, :], ident[:, :])
                    ins.then_inc(cT_ps, 1)

                if s % 2 == 0:
                    scoresT((0, 1))
                    add_c((0, 1))
                    pv(2)
                    scores(0)
                    pv(3)
                    scoresT((2,))
                    project_q_or_v()
                    add_c((2,))
                    scores(1)
                    scoresT((3,))
                    add_c((3,))
                    turn_c()
                    project_k()
                else:
                    scoresT((0, 1))
                    add_c((0, 1))
                    scores(0)
                    project_q_or_v()
                    pv(0)
                    scoresT((2,))
                    add_c((2,))
                    scores(1)
                    scoresT((3,))
                    add_c((3,))
                    pv(1)
                    turn_c()

            def turn_others():
                turn_x(1, range(1, B))

            pe.wait_ge(xT_lo_s, B + 1)
            in_slots(pe, slot, {0: turn_others, 1: lambda: pe.wait_ge(xT_lo_s, 2 * B)})

            for k in range(QT // 2, QT):
                pe.wait_ge(pT_s, QT * (UNITS - 1) + k + 1)
                product((PAIRS - 1) % 2, k)

            def turn_back(b):
                pe.wait_ge(zT_s, b + 1)
                if b >= 2:
                    pe.wait_ge(z_s, b - 1)
                for t in range(QT):
                    ins = T.transpose(psB[b % 2][:, t * P:(t + 1) * P], pT[:, b, t * P:(t + 1) * P],
                                      ident[:, :])
                ins.then_inc(z_ps, 1)

            for b in range(B):
                pe.wait_ge(o_s, PAIRS * (b + 1))
                for h in range(PAIRS):
                    ins = T.matmul(psA[:, b, :], wo[:, h * D:(h + 1) * D],
                                   oT[:, (b * PAIRS + h) * S:(b * PAIRS + h + 1) * S],
                                   start=(h == 0), stop=(h == PAIRS - 1))
                    if h == 0 and b >= 2:
                        turn_x(2, range(b - 2, b - 1))
                    if h == 1 and b >= 1:
                        turn_back(b - 1)
                ins.then_inc(zT_ps, 1)
            turn_back(B - 1)
            turn_x(2, range(B - 2, B - 1))
            ffn(1)


_INS = ['L0_attn_x', 'L0_attn_Wq', 'L0_attn_Wk', 'L0_attn_Wv', 'L0_attn_Wo', 'L0_ffn_router_w',
        'L0_ffn_w1', 'L0_ffn_w2', 'L0_ffn_shared_gate_up', 'L0_ffn_shared_down',
        'L0_ffn_shared_gate_w']


def kernel(**inputs):
    import numpy as _np
    import concourse.bacc as _bacc
    from concourse import mybir as _mybir
    from concourse.bass_utils import run_bass_kernel_spmd as _run

    nc = _bacc.Bacc("TRN2", target_bir_lowering=False, num_devices=1)
    arrays, args = {}, []
    for name in _INS:
        a = _np.ascontiguousarray(inputs[name])
        arrays[f"in_{name}"] = a
        args.append(nc.dram_tensor(f"in_{name}", a.shape, _mybir.dt.from_np(a.dtype),
                                   kind="ExternalInput").ap())
    shape = inputs['L0_attn_x'].shape
    args.append(nc.dram_tensor("out_x", shape, _mybir.dt.float32, kind="ExternalOutput").ap())
    macaron_kernel(nc, *args)
    r = _run(nc, [arrays], core_ids=[0])
    return r.results[0]["out_x"]
```
